# Optimizing a Trainium2 kernel written in Bass

```python
import numpy as np
import jax
import jax.numpy as jnp

def _softmax(x, axis=-1):
    return jax.nn.softmax(x, axis=axis)

def _gelu(x):
    return jax.nn.gelu(x, approximate=True)

def _silu(x):
    return jax.nn.silu(x)

def _sigmoid(x):
    return jax.nn.sigmoid(x)

def _layernorm(x, axis=-1, eps=1e-05):
    m = jnp.mean(x, axis=axis, keepdims=True)
    v = jnp.var(x, axis=axis, keepdims=True)
    return (x - m) / jnp.sqrt(v + eps)

def _scatter_add(tgt, idx, src, axis=0):
    return tgt.at[idx].add(src)

def _segment_sum(src, seg, n):
    return jax.ops.segment_sum(src, seg, n)
kernel_name = 'mk_adj_preln_d2_adj_r2_a82a8f'

def setup_inputs(seed: int=0):
    np.random.seed(seed)
    _w = jnp.asarray

    def _rec_inputs():
        import jax
        import jax.numpy as jnp
        _gk = jax.random.key(seed)
        x = -0.0005207 + 1.001 * jax.random.normal(jax.random.fold_in(_gk, 1), (4096, 256), jnp.float32)
        _a = jax.random.bernoulli(jax.random.fold_in(_gk, 2), 0.00390625, (4096, 4096))
        _a = jnp.logical_or(_a, jnp.swapaxes(_a, -1, -2))
        _a = jnp.logical_or(_a, jnp.eye(4096, dtype=bool))
        _af = _a.astype(jnp.float32)
        _af = _af * jax.random.uniform(jax.random.fold_in(_gk, 3), (4096, 4096), jnp.float32, 0.05, 5.41998)
        adj = _af
        return (x, adj)
    x, adj = _rec_inputs()

    def _L0_gnn_setup():
        import jax, jax.numpy as jnp
        import numpy as np
        N = 2048
        DIM_IN = 256
        DIM_Q = 256
        DIM_K = 256
        N_GRAPHS = 32
        key = jax.random.key(seed)
        ks = jax.random.split(key, 9)
        x = jax.random.normal(ks[0], (N, DIM_IN), dtype=jnp.float32)
        b = jax.random.normal(ks[1], (N, N), dtype=jnp.float32)
        edge_encoding = jax.random.normal(ks[2], (N, N), dtype=jnp.float32)
        ptr = jnp.arange(N_GRAPHS + 1, dtype=jnp.int64) * (N // N_GRAPHS)
        s_in = 1.0 / np.sqrt(DIM_IN)
        Wq = jax.random.normal(ks[3], (DIM_Q, DIM_IN), dtype=jnp.float32) * s_in
        bq = jnp.zeros((DIM_Q,), dtype=jnp.float32)
        Wk = jax.random.normal(ks[4], (DIM_K, DIM_IN), dtype=jnp.float32) * s_in
        bk = jnp.zeros((DIM_K,), dtype=jnp.float32)
        Wv = jax.random.normal(ks[5], (DIM_K, DIM_IN), dtype=jnp.float32) * s_in
        bv = jnp.zeros((DIM_K,), dtype=jnp.float32)
        return {'x': x, 'b': b, 'edge_encoding': edge_encoding, 'ptr': ptr, 'Wq': Wq, 'bq': bq, 'Wk': Wk, 'bk': bk, 'Wv': Wv, 'bv': bv}
    _L0_gnn_all = _L0_gnn_setup()
    _L0_gnn_in = {k: v for k, v in _L0_gnn_all.items() if k in ('ptr', 'Wq', 'bq', 'Wk', 'bk', 'Wv', 'bv')}
    del _L0_gnn_all

    def _L1_gnn_setup():
        import jax, jax.numpy as jnp
        import numpy as np
        KAPPA = -1.0
        EPS = 1e-10
        N, D_IN, D_OUT = (4096, 256, 256)

        def _artan_k(x):
            sc = np.sqrt(-KAPPA)
            return jnp.arctanh(jnp.clip(sc * x, -1.0 + 1e-07, 1.0 - 1e-07)) / sc

        def _tan_k(x):
            sc = np.sqrt(-KAPPA)
            return jnp.tanh(sc * x) / sc

        def _clamp_abs(x, eps=EPS):
            return jnp.where(x >= 0, 1.0, -1.0) * jnp.maximum(jnp.abs(x), eps)

        def _norm(x):
            return jnp.sqrt(jnp.maximum(jnp.sum(x * x, axis=-1, keepdims=True), EPS * EPS))

        def mobius_matvec(W, x):
            x_norm = _norm(x)
            mx = x @ W
            mx_norm = _norm(mx)
            res = _tan_k(mx_norm / x_norm * _artan_k(x_norm)) * (mx / mx_norm)
            return jnp.where(mx_norm <= EPS, 0.0, res)

        def mobius_scalar_mul(r, x):
            x_norm = _norm(x)
            return _tan_k(r * _artan_k(x_norm)) * (x / x_norm)

        def weighted_midpoint_lincomb(A, X):
            gamma = jnp.maximum(2.0 / (1.0 + KAPPA * jnp.sum(X * X, axis=-1, keepdims=True)), 1e-15)
            denom = _clamp_abs(A @ (gamma - 1.0))
            nom = A @ (gamma * X)
            two_mean = nom / denom
            sq = jnp.sum(two_mean * two_mean, axis=-1, keepdims=True)
            a_mean = two_mean / (1.0 + jnp.sqrt(jnp.maximum(1.0 + KAPPA * sq, EPS)))
            alpha = jnp.sum(A, axis=-1, keepdims=True)
            return mobius_scalar_mul(alpha, a_mean)

        def logmap0(x):
            xn = _norm(x)
            return _artan_k(xn) * x / xn

        def expmap0(u):
            un = _norm(u)
            return _tan_k(un) * u / un
        key = jax.random.key(seed)
        k1, k2, k3 = jax.random.split(key, 3)
        X = jax.random.normal(k1, (N, D_IN), dtype=jnp.float32) * 0.001
        A_hat = jax.random.uniform(k2, (N, N), dtype=jnp.float32) / N
        W = jax.random.normal(k3, (D_IN, D_OUT), dtype=jnp.float32) * 0.01
        return {'X': X, 'A_hat': A_hat, 'W': W}
    _L1_gnn_all = _L1_gnn_setup()
    _L1_gnn_in = {k: v for k, v in _L1_gnn_all.items() if k in ('W',)}
    del _L1_gnn_all
    return {'x': x, 'adj': adj, 'L0_gnn_ptr': _L0_gnn_in['ptr'], 'L0_gnn_Wq': _L0_gnn_in['Wq'], 'L0_gnn_bq': _L0_gnn_in['bq'], 'L0_gnn_Wk': _L0_gnn_in['Wk'], 'L0_gnn_bk': _L0_gnn_in['bk'], 'L0_gnn_Wv': _L0_gnn_in['Wv'], 'L0_gnn_bv': _L0_gnn_in['bv'], 'L1_gnn_W': _L1_gnn_in['W']}

def reference(x, adj, L0_gnn_ptr, L0_gnn_Wq, L0_gnn_bq, L0_gnn_Wk, L0_gnn_bk, L0_gnn_Wv, L0_gnn_bv, L1_gnn_W):
    import jax
    import jax.numpy as jnp

    def _L0_gnn_ref(x, b, edge_encoding, ptr, Wq, bq, Wk, bk, Wv, bv):
        import jax, jax.numpy as jnp
        import numpy as np
        N = 2048
        DIM_IN = 256
        DIM_Q = 256
        DIM_K = 256
        N_GRAPHS = 32
        n = x.shape[0]
        graph_id = jnp.searchsorted(ptr, jnp.arange(n), side='right') - 1
        mask = graph_id[:, None] == graph_id[None, :]
        query = x @ Wq.T + bq
        key = x @ Wk.T + bk
        value = x @ Wv.T + bv
        scale = 1.0 / jnp.sqrt(jnp.float32(query.shape[-1]))
        a = jnp.where(mask, query @ key.T * scale, 0.0)
        scores = (a + b + edge_encoding) * jnp.where(mask, 1.0, -1000000.0)
        softmax = jax.nn.softmax(scores, axis=-1) * mask
        return softmax @ value

    def _L1_gnn_ref(X, A_hat, W):
        import jax, jax.numpy as jnp
        import numpy as np
        KAPPA = -1.0
        EPS = 1e-10
        N, D_IN, D_OUT = (4096, 256, 256)

        def _artan_k(x):
            sc = np.sqrt(-KAPPA)
            return jnp.arctanh(jnp.clip(sc * x, -1.0 + 1e-07, 1.0 - 1e-07)) / sc

        def _tan_k(x):
            sc = np.sqrt(-KAPPA)
            return jnp.tanh(sc * x) / sc

        def _clamp_abs(x, eps=EPS):
            return jnp.where(x >= 0, 1.0, -1.0) * jnp.maximum(jnp.abs(x), eps)

        def _norm(x):
            return jnp.sqrt(jnp.maximum(jnp.sum(x * x, axis=-1, keepdims=True), EPS * EPS))

        def mobius_matvec(W, x):
            x_norm = _norm(x)
            mx = x @ W
            mx_norm = _norm(mx)
            res = _tan_k(mx_norm / x_norm * _artan_k(x_norm)) * (mx / mx_norm)
            return jnp.where(mx_norm <= EPS, 0.0, res)

        def mobius_scalar_mul(r, x):
            x_norm = _norm(x)
            return _tan_k(r * _artan_k(x_norm)) * (x / x_norm)

        def weighted_midpoint_lincomb(A, X):
            gamma = jnp.maximum(2.0 / (1.0 + KAPPA * jnp.sum(X * X, axis=-1, keepdims=True)), 1e-15)
            denom = _clamp_abs(A @ (gamma - 1.0))
            nom = A @ (gamma * X)
            two_mean = nom / denom
            sq = jnp.sum(two_mean * two_mean, axis=-1, keepdims=True)
            a_mean = two_mean / (1.0 + jnp.sqrt(jnp.maximum(1.0 + KAPPA * sq, EPS)))
            alpha = jnp.sum(A, axis=-1, keepdims=True)
            return mobius_scalar_mul(alpha, a_mean)

        def logmap0(x):
            xn = _norm(x)
            return _artan_k(xn) * x / xn

        def expmap0(u):
            un = _norm(u)
            return _tan_k(un) * u / un
        XW = mobius_matvec(W, X)
        AXW = weighted_midpoint_lincomb(A_hat, XW)
        return expmap0(jax.nn.relu(logmap0(AXW)))
    h = jnp.maximum(_layernorm(x, axis=-1), 0.0)
    x = x + _L0_gnn_ref(h, adj, adj, L0_gnn_ptr, L0_gnn_Wq, L0_gnn_bq, L0_gnn_Wk, L0_gnn_bk, L0_gnn_Wv, L0_gnn_bv)
    h = jnp.maximum(_layernorm(x, axis=-1), 0.0)
    x = x + _L1_gnn_ref(h, adj, L1_gnn_W)
    return x

_drawn_inputs = setup_inputs


def setup_inputs(seed=0):
    import zlib

    import numpy as np

    out = dict(_drawn_inputs(seed))
    spreads = {'L0_gnn_bq': (0.0, 0.8), 'L0_gnn_bk': (0.0, 0.8), 'L0_gnn_bv': (0.0, 0.1)}
    factors = {}
    for name, (base, spread) in spreads.items():
        noise = np.random.default_rng([zlib.crc32(name.encode()), seed]).standard_normal(out[name].shape)
        drawn = base * np.exp(spread * noise) if base else spread * noise
        out[name] = jnp.asarray(drawn.astype(out[name].dtype))
    for name, factor in factors.items():
        out[name] = (out[name] * factor).astype(out[name].dtype)
    return out
```

```python
import concourse.bass as bass
from concourse import mybir
from contextlib import ExitStack

F32 = mybir.dt.float32
BF16 = mybir.dt.bfloat16
I32 = mybir.dt.int32
ALU = mybir.AluOpType
ACT = mybir.ActivationFunctionType
AX = mybir.AxisListType

P = 128
LN_EPS = 1e-5
FAR = -1.0e6
FLOOR = 1e-20
EPS = 1e-10
CLIP = 1.0 - 1e-7
TINY_ARG = 0.25
PUSHED_OUT = 1.0e30


POINT_FUNCTIONS = [(ACT.Sqrt, 0), (ACT.Sqrt, 1), (ACT.Sqrt, 2), (ACT.Ln, 5), (ACT.Tanh, 3)]
FINISH_FUNCTIONS = [(ACT.Sqrt, 0), (ACT.Sqrt, 1), (ACT.Ln, 5), (ACT.Tanh, 2), (ACT.Sqrt, 1), (ACT.Ln, 5),
                    (ACT.Sqrt, 1), (ACT.Tanh, 1)]


def graph_layers_kernel(nc, x, adj, ptr, Wq, bq, Wk, bk, Wv, bv, W, out):
    N, D = x.shape
    T = N // P
    HT = T // 2
    KD = D // P
    CH = 512
    BPC = CH // P
    NG = N // CH
    HALF = N // 2
    HC = HALF // CH
    NPTR = ptr.shape[0]
    XW = D + 2
    HALF_SCALE = 0.5 / float(D) ** 0.5

    x_g = x.rearrange("(g j p) d -> g p j d", p=P, j=BPC)
    x_t = x.rearrange("(t p) d -> t p d", p=P)
    adj_t = adj.rearrange("(t p) n -> t p n", p=P)
    out_g = out.rearrange("(g j p) d -> g p j d", p=P, j=BPC)

    ctx = ExitStack()
    with ctx:
        def sb(name, shape, dt=F32):
            return ctx.enter_context(nc.sbuf_tensor(name, shape, dt))

        def sem(name):
            return ctx.enter_context(nc.semaphore(name))

        x1_dram = nc.dram_tensor("x1_scratch", [N, D], F32, kind="Internal").ap()
        x1_t = x1_dram.rearrange("(t p) d -> t p d", p=P)
        x1_g = x1_dram.rearrange("(g j p) d -> g p j d", p=P, j=BPC)

        keysT = sb("keysT", [P, KD, N])
        values = sb("values", [P, T, D])
        qx = sb("qx", [P, T, XW])
        graph_row = sb("graph_row", [P, N], BF16)
        adjU = sb("adjU", [P, 2, N])
        adjL = sb("adjL", [P, N])
        scores = sb("scores", [P, 2, HALF])
        hT = sb("hT", [P, 2, KD, CH])
        xin = sb("xin", [P, 2, BPC, D])
        wT = sb("wT", [P, 3, KD, D])
        w1 = sb("w1", [P, KD, D])
        bqk = sb("bqk", [P, 2, KD])
        bv_row = sb("bv_row", [P, 2, D])
        probT = sb("probT", [P, 2, BPC, P])
        xt = sb("xt", [P, 2, D])
        x1 = sb("x1", [P, 2, D])
        cent = sb("cent", [P, 2, D])
        centT = sb("centT", [P, 2, KD, P])
        junk = sb("junk", [P, 4, D], BF16)
        qst = sb("qst", [P, 2, KD, P])
        own = sb("own", [P, 2, P])
        same = sb("same", [P, 2, P])
        factor = sb("factor", [P, P])
        far_part = sb("far_part", [P, P])
        near_part = sb("near_part", [P, P])
        ident = sb("ident", [P, P])
        ident_b = sb("ident_b", [P, P], BF16)
        ones_b = sb("ones_b", [P, P], BF16)
        pushed = sb("pushed", [P, P])
        diag = sb("diag", [P, 2, CH], BF16)
        graph_col = sb("graph_col", [P, T])
        row_no = sb("row_no", [P, T])
        row_no_i = sb("row_no_i", [P, T], I32)
        ptr_i = sb("ptr_i", [P, NPTR], I32)
        ptr_f = sb("ptr_f", [P, NPTR])
        in_upper = sb("in_upper", [P, NPTR])
        below_end = sb("below_end", [P, NPTR])
        borders = sb("borders", [P, HT])
        border_hit = sb("border_hit", [P, HT])
        checks = sb("checks", [P, 4])
        fast = sb("fast", [P, 1], I32)
        ln_eps = sb("ln_eps", [P, 1])
        bnst = sb("bnst", [P, BPC, 6])
        mv = sb("mv", [P, BPC, 2])
        rstd = sb("rstd", [P, BPC])
        mx = sb("mx", [P, 8])
        top = sb("top", [P, 1])
        least = sb("least", [P, 1])
        neg_top = sb("neg_top", [P, 2, 2])
        esum = sb("esum", [P, 2, 2, 2])
        tot = sb("tot", [P, 2])
        bn1 = sb("bn1", [P, 6])
        mv1 = sb("mv1", [P, 2])
        var_all = sb("var_all", [P, T])
        cent_sq = sb("cent_sq", [P, T])
        mx_sq = sb("mx_sq", [P, T])
        sq2 = sb("sq2", [P, 4])
        tm_sq = sb("tm_sq", [P, T])
        r_sq = sb("r_sq", [P, T])
        alpha = sb("alpha", [P, T])
        v = [sb(f"v{i}", [P, T]) for i in range(9)]
        rec = sb("rec", [P, 2])
        sgn = sb("sgn", [P, 2])
        size = sb("size", [P, 2])
        turn = sb("turn", [P, 2])

        w_raw = scores[:, 0, 0:3 * KD * D].rearrange("p (w h d) -> p w h d", w=3, h=KD)
        counts = scores[:, 1, 0:T * NPTR].rearrange("p (t k) -> p t k", k=NPTR)
        border_eq = adjL[:, 0:HT * NPTR].rearrange("p (t k) -> p t k", k=NPTR)
        adjT = scores[:, 0, :].rearrange("p (r b c) -> p r b c", r=4, b=BPC)
        nom = scores[:, 1, 0:2 * XW].rearrange("p (s c) -> p s c", s=2)
        res = values
        x1_all = keysT[:, :, :].rearrange("p k n -> p (k n)").rearrange("p (t d) -> p t d", d=D)
        mask_c = scores[:, 0, 0:CH]
        factor_c = scores[:, 0, CH:2 * CH]
        near_c = scores[:, 0, 2 * CH:3 * CH]

        qx_v = qx[:, :, :].rearrange("p (g j) c -> p g j c", j=BPC)
        val_v = values[:, :, :].rearrange("p (g j) d -> p g j d", j=BPC)
        keys_g = keysT[:, :, :].rearrange("p k (g c) -> p k g c", c=CH)
        keys_t = keysT[:, :, :].rearrange("p k (t c) -> p k t c", c=P)
        graph_t = graph_row[:, :].rearrange("p (t c) -> p t c", c=P)
        adjL_t = adjL[:, :].rearrange("p (t c) -> p t c", c=P)

        bank = [ctx.enter_context(nc.psum_tensor(f"bank{i}", [P, CH], F32)) for i in range(8)]

        s_ptr = sem("ptr_in")
        s_w = sem("weights_in")
        s_xin = [sem("x_group_in0"), sem("x_group_in1")]
        s_ident = sem("ident_ready")
        s_rows = sem("row_numbers_ready")
        s_const = sem("vector_constants_ready")
        s_setup = sem("vector_setup_steps")
        s_wt_ps = sem("weights_turned")
        s_wt = sem("turned_weights_copied")
        s_diag = sem("diag_ready")
        s_grow_ps = sem("graph_row_in_psum")
        s_grow = sem("graph_row_copied")
        s_fast = sem("path_chosen")
        s_var = sem("variance_ready")
        s_std = sem("deviation_ready")
        s_norm = sem("normalised")
        s_hT_ps = sem("h_turned")
        s_hT = sem("hT_copied")
        s_kq_ps = sem("keys_queries_in_psum")
        s_kq = sem("keys_queries_copied")
        s_v_ps = sem("values_in_psum")
        s_v = sem("values_copied")
        s_adjU = [sem("adj_upper_in0"), sem("adj_upper_in1")]
        s_adjL = sem("adj_lower_in")
        s_xt = [sem("x_tile_in0"), sem("x_tile_in1")]
        s_x1_out = [sem("x1_stored0"), sem("x1_stored1")]
        s_q = sem("queries_staged")
        s_qkU = sem("upper_scores_in_psum")
        s_qkU_used = sem("upper_scores_read")
        s_seen = sem("upper_scores_seen")
        s_qkL = sem("lower_scores_in_psum")
        s_qkL_used = sem("lower_scores_read")
        s_maxU = sem("upper_maximum_ready")
        s_maxL = sem("lower_maximum_ready")
        s_expU = sem("upper_exp_done")
        s_expL = sem("lower_exp_done")
        s_pT_ps = sem("exp_turned")
        s_pT = sem("turned_exp_copied")
        s_pTL = sem("lower_turned_exp_copied")
        s_pv = sem("group_of_values_summed")
        s_x1 = sem("x1_ready")
        s_cent = sem("centred_ready")
        s_cT_ps = sem("centred_turned")
        s_cT = sem("centred_copied")
        s_mx_ps = sem("product_in_psum")
        s_mx = sem("product_copied")
        g_adj = sem("general_adj_in")
        g_qk = sem("general_scores_in_psum")
        g_qk_used = sem("general_scores_read")
        g_max = sem("general_maximum_ready")
        g_exp = sem("general_exp_done")
        g_mask = sem("general_exp_masked")
        s_var_in = sem("statistics_complete")
        s_f = sem("factor_step")
        s_fa = sem("factor_function")
        s_pts = sem("points_ready")
        s_ptsA = sem("points_ready_scalar")
        d_adj = [sem("mean_adj_in0"), sem("mean_adj_in1")]
        d_t_ps = sem("adj_turned")
        d_tA = sem("turned_adj_copied_scalar")
        d_tV = sem("turned_adj_copied_vector")
        d_mm = sem("group_of_mean_summed")
        d_nom = sem("mean_copied")
        d_rec = sem("denominator_ready")
        d_r = sem("mean_relu_ready")
        d_sq = sem("mean_squares_ready")
        s_x1_all = sem("x1_back")
        s_out = sem("out_group_ready")
        s_stored = sem("out_stored")

        def wait(eng, s, value):
            if not isinstance(value, int) or value > 0:
                eng.wait_ge(s, value)

        def always(eng):
            eng.wait_ge(s_ident, 3)

        def pipeline(eng, n, step):
            step(0, 0)
            with eng.Fori(0, (n - 2) // 2) as i:
                step(2 * i + 1, 1)
                step(2 * i + 2, 0)
            step(n - 1, 1)

        block = ctx.enter_context(nc.Block())

        @block.sync
        def _(sp):
            sp.dma_start(ptr_i[:, :], ptr.rearrange("(a k) -> a k", a=1).partition_broadcast(P)).then_inc(s_ptr, 16)
            sp.dma_start(xin[:, 0], x_g[0]).then_inc(s_xin[0], 16)
            for n, w in enumerate((Wq, Wk, Wv)):
                sp.dma_start(w_raw[:, n], w.rearrange("(h p) d -> p h d", p=P)).then_inc(s_w, 16)
            with nc.allow_non_contiguous_dma(reason="biases, one column each"):
                sp.dma_start(bqk[:, 0], bq.rearrange("(h p) -> p h", p=P)).then_inc(s_w, 16)
                sp.dma_start(bqk[:, 1], bk.rearrange("(h p) -> p h", p=P)).then_inc(s_w, 16)
            for j in range(2):
                sp.dma_start(bv_row[:, j], bv.rearrange("(a d) -> a d", a=1).partition_broadcast(P)).then_inc(s_w, 16)
            sp.dma_start(w1[:, :, :], W.rearrange("(k p) d -> p k d", p=P)).then_inc(s_w, 16)
            sp.dma_start(xin[:, 1], x_g[1]).then_inc(s_xin[1], 16)

            def x_group(g, par):
                sp.wait_ge(s_hT_ps, g - 1)
                sp.dma_start(xin[:, par], x_g[g]).then_inc(s_xin[par], 16)

            with sp.Fori(0, (NG - 2) // 2) as i:
                x_group(2 * i + 2, 0)
                x_group(2 * i + 3, 1)

            def x_tile(s, n, slot, t):
                wait(sp, s_x1, n - 1)
                sp.dma_start(xt[:, slot], x_t[t]).then_inc(s_xt[slot], 16)

            def x1_store(n, slot, t):
                sp.wait_ge(s_x1, n + 1)
                sp.dma_start(x1_t[t], x1[:, slot]).then_inc(s_x1_out[slot], 16)

            sp.wait_ge(s_fast, 1)
            flag = sp.value_load(fast[0:1, 0:1], min_val=0, max_val=1)
            with sp.If(flag > 0):
                sp.dma_start(adjU[:, 0], adj_t[HT]).then_inc(s_adjU[0], 16)
                sp.dma_start(adjL[:, :], adj_t[0]).then_inc(s_adjL, 16)

                def step(s, par):
                    last = isinstance(s, int) and s == HT - 1
                    if not last:
                        wait(sp, s_expU, s)
                        sp.dma_start(adjU[:, 1 - par], adj_t[s + HT + 1]).then_inc(s_adjU[1 - par], 16)
                        sp.wait_ge(s_expL, s + 1)
                        sp.dma_start(adjL[:, :], adj_t[s + 1]).then_inc(s_adjL, 16)
                    if not (isinstance(s, int) and s == 0):
                        x1_store(2 * s - 2, 0, s - 1 + HT)
                        x1_store(2 * s - 1, 1, s - 1)
                    x_tile(s, 2 * s, 0, s + HT)
                    x_tile(s, 2 * s + 1, 1, s)

                pipeline(sp, HT, step)
                x1_store(T - 2, 0, T - 1)
                x1_store(T - 1, 1, HT - 1)
            with sp.Else():
                def pair(s, par):
                    for slot in range(2):
                        n = 2 * s + slot
                        wait(sp, s_pT_ps, n * NG)
                        sp.dma_start(adjU[:, 0], adj_t[n]).then_inc(g_adj, 16)
                        x_tile(s, n, slot, n)
                        x1_store(n, slot, n)

                pipeline(sp, HT, pair)

            for slot in range(2):
                sp.wait_ge(s_x1_out[slot], 16 * HT)
            sp.wait_ge(s_mx, T + 2)
            sp.dma_start(adjU[:, 0], adj_t[0]).then_inc(d_adj[0], 16)
            sp.dma_start(adjU[:, 1], adj_t[1]).then_inc(d_adj[1], 16)
            for g in range(0, NG, 4):
                sp.dma_start(x1_all[:, g * BPC:(g + 4) * BPC, :],
                             x1_dram[g * CH:(g + 4) * CH, :].rearrange("(t p) d -> p t d", p=P)).then_inc(s_x1_all, 16)
            with sp.Fori(0, HT - 1) as i:
                for par in range(2):
                    t = 2 * i + par
                    sp.wait_ge(d_t_ps, NG * t + NG)
                    sp.dma_start(adjU[:, par], adj_t[t + 2]).then_inc(d_adj[par], 16)
            for g in range(NG):
                sp.wait_ge(s_out, g + 1)
                sp.dma_start(out_g[g], res[:, g * BPC:(g + 1) * BPC, :]).then_inc(s_stored, 16)
            sp.wait_ge(s_stored, 16 * NG)

        @block.gpsimd
        def _(pool):
            pool.iota(row_no_i[:, :], pattern=[[P, T]], base=0, channel_multiplier=1).then_inc(s_rows, 1)
            pool.memset(ident[:, :], 0.0).then_inc(s_ident, 1)
            pool.memset(ones_b[:, :], 1.0).then_inc(s_ident, 1)
            pool.wait_ge(s_ident, 2)
            pool.affine_select(out=ident[:, :], in_=ident[:, :], compare_op=ALU.not_equal, fill=1.0, base=0,
                               pattern=[[-1, P]], channel_multiplier=1).then_inc(s_ident, 1)

            pool.wait_ge(s_kq, 2 * KD * NG)
            pool.wait_ge(s_fast, 1)
            flag = pool.value_load(fast[0:1, 0:1], min_val=0, max_val=1)
            with pool.If(flag > 0):
                def step(s, par):
                    wait(pool, s_qkL, s)
                    always(pool)
                    pool.tensor_copy(qst[:, 0].rearrange("p k c -> p (k c)"), qx[:, s + HT, 0:D]).then_inc(s_q, 1)
                    always(pool)
                    pool.tensor_copy(qst[:, 1].rearrange("p k c -> p (k c)"), qx[:, s, 0:D]).then_inc(s_q, 1)

                pipeline(pool, HT, step)
            with pool.Else():
                def pair(s, par):
                    for slot in range(2):
                        n = 2 * s + slot
                        wait(pool, g_qk, NG * (n - 1))
                        always(pool)
                        pool.tensor_copy(qst[:, slot].rearrange("p k c -> p (k c)"), qx[:, n, 0:D]).then_inc(s_q, 1)

                pipeline(pool, HT, pair)

        @block.tensor
        def _(pe):
            pe.wait_ge(s_ident, 3)
            pe.wait_ge(s_w, 16 * 8)
            for n in range(3):
                for h in range(KD):
                    for k in range(KD):
                        last = pe.transpose(bank[n][:, k * D + h * P:k * D + (h + 1) * P],
                                            w_raw[:, n, h, k * P:(k + 1) * P], ident[:, :])
                last.then_inc(s_wt_ps, 1)
            for g in range(NG):
                pe.wait_ge(s_diag, g + 1)
                wait(pe, s_grow, g - 1)
                pe.matmul(bank[3 + g % 2][:, :], ones_b[:, :], diag[:, g % 2, :], start=True, stop=True)\
                  .then_inc(s_grow_ps, 1)

            def turn_h(g, par):
                pe.wait_ge(s_norm, g + 1)
                wait(pe, s_hT, KD * g)
                for k in range(KD):
                    for j in range(BPC):
                        last = pe.transpose(bank[k][:, j * P:(j + 1) * P], xin[:, par, j, k * P:(k + 1) * P],
                                            ident[:, :])
                last.then_inc(s_hT_ps, 1)

            def project(g, par):
                pe.wait_ge(s_hT, KD * (g + 1))
                for w in range(2):
                    for h in range(KD):
                        i = w * KD + h
                        wait(pe, s_kq, 4 * g + i - 3)
                        for k in range(KD):
                            last = pe.matmul(bank[2 + i][:, :], wT[:, w, k, h * P:(h + 1) * P], hT[:, par, k, :],
                                             start=(k == 0), stop=(k == KD - 1))
                        last.then_inc(s_kq_ps, 1)

                if not (isinstance(g, int) and g == NG - 1):
                    turn_h(g + 1, 1 - par)
                for b in range(2):
                    wait(pe, s_v, 2 * g + b - 1)
                    for j in range(2):
                        for k in range(KD):
                            last = pe.matmul(bank[6 + b][:, j * D:(j + 1) * D],
                                             hT[:, par, k, (2 * b + j) * P:(2 * b + j + 1) * P], wT[:, 2, k, :],
                                             start=(k == 0), stop=(k == KD - 1))
                    last.then_inc(s_v_ps, 1)

            pe.wait_ge(s_grow, NG)
            pe.wait_ge(s_wt, 3)
            turn_h(0, 0)
            pipeline(pe, NG, project)
            pe.wait_ge(s_kq, 4 * NG)
            pe.wait_ge(s_v, 2 * NG)

            def product(s):
                pe.wait_ge(s_cent, 2 * s + 2)
                pe.wait_ge(s_mx, 2 * s + 2)
                for slot in range(2):
                    for k in range(KD):
                        last = pe.transpose(bank[7][:, (slot * KD + k) * P:(slot * KD + k + 1) * P],
                                            cent[:, slot, k * P:(k + 1) * P], ident[:, :])
                last.then_inc(s_cT_ps, 1)
                pe.wait_ge(s_cT, s + 1)
                for slot in range(2):
                    for k in range(KD):
                        last = pe.matmul(bank[7][:, slot * D:(slot + 1) * D], centT[:, slot, k, :], w1[:, k, :],
                                         start=(k == 0), stop=(k == KD - 1))
                last.then_inc(s_mx_ps, 1)

            flag = pe.value_load(fast[0:1, 0:1], min_val=0, max_val=1)
            with pe.If(flag > 0):
                def scores_of(s):
                    pe.wait_ge(s_q, 2 * s + 2)
                    for c in range(HC):
                        wait(pe, s_qkU_used, HC * s + c - 1)
                        for k in range(KD):
                            last = pe.matmul(bank[1 + c % 2][:, :], qst[:, 0, k, :], keys_g[:, k, HC + c, :],
                                             start=(k == 0), stop=(k == KD - 1))
                        last.then_inc(s_qkU, 1)
                    wait(pe, s_qkL_used, s)
                    for k in range(KD):
                        last = pe.matmul(bank[0][:, 0:P], qst[:, 1, k, :], keys_t[:, k, s, :],
                                         start=(k == 0), stop=(k == KD - 1))
                    last.then_inc(s_qkL, 1)

                def turn(s, par, c):
                    b = (par * (HC + 1) + c) % 2
                    if c < HC:
                        if c == 0:
                            pe.wait_ge(s_expU, s + 1)
                            wait(pe, s_pT, HC * s)
                        elif c == 1:
                            wait(pe, s_pTL, s)
                        else:
                            pe.wait_ge(s_pT, HC * s + c - 1)
                        for j in range(BPC):
                            last = pe.transpose(bank[3 + b][:, j * P:(j + 1) * P],
                                                scores[:, par, (c * BPC + j) * P:(c * BPC + j + 1) * P], ident[:, :])
                    else:
                        pe.wait_ge(s_expL, s + 1)
                        pe.wait_ge(s_pT, HC * s + c - 1)
                        last = pe.transpose(bank[3 + b][:, 0:P], own[:, par, :], ident[:, :])
                    last.then_inc(s_pT_ps, 1)

                def weigh(s, par, c):
                    b = (par * (HC + 1) + c) % 2
                    if c < HC:
                        pe.wait_ge(s_pT, HC * s + c + 1)
                        if c == 0:
                            wait(pe, s_x1, 2 * s - 1)
                        for j in range(BPC):
                            last = pe.matmul(bank[5][:, 0:D], probT[:, b, j, :], values[:, HT + c * BPC + j, :],
                                             start=(c == 0 and j == 0), stop=(c == HC - 1 and j == BPC - 1))
                        last.then_inc(s_pv, 1)
                    else:
                        pe.wait_ge(s_pTL, s + 1)
                        wait(pe, s_x1, 2 * s)
                        pe.matmul(bank[6][:, 0:D], probT[:, b, 0, :], values[:, s, :], start=True, stop=True)\
                          .then_inc(s_pv, 1)

                def step(s, par):
                    if not (isinstance(s, int) and s == HT - 1):
                        scores_of(s + 1)
                    if not (isinstance(s, int) and s == 0):
                        product(s - 1)
                    turn(s, par, 0)
                    for c in range(HC + 1):
                        if c < HC:
                            turn(s, par, c + 1)
                        weigh(s, par, c)

                scores_of(0)
                pipeline(pe, HT, step)
                product(HT - 1)
            with pe.Else():
                def pair(s, par):
                    for slot in range(2):
                        n = 2 * s + slot
                        pe.wait_ge(s_q, n + 1)
                        for c in range(NG):
                            wait(pe, g_qk_used, NG * n + c - 1)
                            for k in range(KD):
                                last = pe.matmul(bank[1 + c % 2][:, :], qst[:, slot, k, :], keys_g[:, k, c, :],
                                                 start=(k == 0), stop=(k == KD - 1))
                            last.then_inc(g_qk, 1)
                        pe.wait_ge(g_mask, n + 1)
                        for c in range(NG):
                            wait(pe, s_pT, NG * n + c - 1)
                            for j in range(BPC):
                                last = pe.transpose(bank[3 + c % 2][:, j * P:(j + 1) * P],
                                                    adjU[:, 0, (c * BPC + j) * P:(c * BPC + j + 1) * P], ident[:, :])
                            last.then_inc(s_pT_ps, 1)
                            pe.wait_ge(s_pT, NG * n + c + 1)
                            if c == 0:
                                wait(pe, s_x1, n - 1)
                            for j in range(BPC):
                                last = pe.matmul(bank[5 + slot][:, 0:D], probT[:, c % 2, j, :],
                                                 values[:, c * BPC + j, :],
                                                 start=(c == 0 and j == 0), stop=(c == NG - 1 and j == BPC - 1))
                            last.then_inc(s_pv, 1)
                    product(s)

                pipeline(pe, HT, pair)

            pe.wait_ge(s_mx, T + 2)

            def turn_adj(t, par, g):
                if g == 0:
                    pe.wait_ge(d_adj[par], 16 * ((t - par) // 2 + 1) if isinstance(t, int) else t * 8 - 8 * par + 16)
                wait(pe, d_tA if g % 2 == 0 else d_tV, NG // 2 * t + g // 2 - 1)
                for j in range(BPC):
                    last = pe.transpose(bank[g % 4][:, j * P:(j + 1) * P],
                                        adjU[:, par, (g * BPC + j) * P:(g * BPC + j + 1) * P], ident[:, :])
                last.then_inc(d_t_ps, 1)

            def mean_part(t, par, g):
                if g == 0:
                    wait(pe, d_nom, t)
                pe.wait_ge(d_tA if g % 2 == 0 else d_tV, NG // 2 * t + g // 2 + 1)
                for j in range(BPC):
                    last = pe.matmul(bank[4 + par][:, 0:XW], adjT[:, g % 4, j, :], qx[:, g * BPC + j, :],
                                     start=(g == 0 and j == 0), stop=(g == NG - 1 and j == BPC - 1))
                last.then_inc(d_mm, 1)

            def mean_tile(t, par):
                for g in range(NG):
                    turn_adj(t, par, g)
                    if g >= 2:
                        if g == 2 and isinstance(t, int) and t == 0:
                            pe.wait_ge(s_pts, 1)
                            pe.wait_ge(s_ptsA, 1)
                        mean_part(t, par, g - 2)
                    elif not (isinstance(t, int) and t == 0):
                        mean_part(t - 1, 1 - par, NG - 2 + g)

            pipeline(pe, T, mean_tile)
            mean_part(T - 1, 1, NG - 2)
            mean_part(T - 1, 1, NG - 1)

        @block.scalar
        def _(act):
            act.sem_inc(s_mx, 2)
            act.sem_inc(d_nom, 1)
            for n in range(3):
                act.wait_ge(s_wt_ps, n + 1)
                act.copy(wT[:, n].rearrange("p k d -> p (k d)"), bank[n][:, :]).then_inc(s_wt, 1)
            for g in range(NG):
                act.wait_ge(s_grow_ps, g + 1)
                act.copy(graph_row[:, g * CH:(g + 1) * CH], bank[3 + g % 2][:, :]).then_inc(s_grow, 1)

            def deviation(g):
                act.wait_ge(s_var, g + 1)
                act.activation(rstd[:, :], mv[:, :, 1], ACT.Sqrt, bias=ln_eps[:, 0:1]).then_inc(s_std, 1)

            def relu_h(g, par):
                act.wait_ge(s_hT_ps, g + 1)
                wait(act, s_v_ps, 2 * g - 2)
                for k in range(KD):
                    act.activation(hT[:, par, k, :], bank[k][:, :], ACT.Relu).then_inc(s_hT, 1)

            def keys_queries(g):
                for w in range(2):
                    for h in range(KD):
                        act.wait_ge(s_kq_ps, 4 * g + w * KD + h + 1)
                        always(act)
                        src = bank[2 + w * KD + h][:, :].rearrange("p (j c) -> p j c", j=BPC)
                        if w == 0:
                            ins = act.activation(qx_v[:, g, :, h * P:(h + 1) * P], src, ACT.Identity,
                                                 bias=bqk[:, 0, h:h + 1], scale=HALF_SCALE)
                        else:
                            ins = act.activation(keys_g[:, h, g, :], bank[2 + w * KD + h][:, :], ACT.Identity,
                                                 bias=bqk[:, 1, h:h + 1])
                        ins.then_inc(s_kq, 1)

            def project(g, par):
                more = not (isinstance(g, int) and g == NG - 1)
                if more:
                    deviation(g + 1)
                keys_queries(g)
                if more:
                    relu_h(g + 1, 1 - par)

            act.wait_ge(s_const, 1)
            deviation(0)
            relu_h(0, 0)
            pipeline(act, NG, project)

            def finish_product(s, tiles):
                for slot in range(2):
                    act.wait_ge(s_cent, 2 * s + slot + 1)
                    act.activation(junk[:, slot], cent[:, slot], ACT.Square, accum_out=sq2[:, slot:slot + 1])
                act.wait_ge(s_cT_ps, s + 1)
                act.copy(centT[:, :, :, :].rearrange("p s k c -> p (s k c)"), bank[7][:, :]).then_inc(s_cT, 1)
                act.wait_ge(s_mx_ps, s + 1)
                for slot in range(2):
                    act.activation(junk[:, 2 + slot], bank[7][:, slot * D:(slot + 1) * D], ACT.Square,
                                   accum_out=sq2[:, 2 + slot:3 + slot])
                act.drain()
                for slot in range(2):
                    act.copy(cent_sq[:, bass.ds(tiles[slot], 1)], sq2[:, slot:slot + 1])
                    act.copy(mx_sq[:, bass.ds(tiles[slot], 1)], sq2[:, 2 + slot:3 + slot])
                    act.copy(qx[:, tiles[slot], 0:D], bank[7][:, slot * D:(slot + 1) * D]).then_inc(s_mx, 1)

            act.wait_ge(s_fast, 1)
            flag = act.value_load(fast[0:1, 0:1], min_val=0, max_val=1)
            with act.If(flag > 0):
                def exps(s, par):
                    act.wait_ge(s_maxU, s + 1)
                    act.activation(adjU[:, par, 0:HALF], adjU[:, par, 0:HALF], ACT.Exp, scale=2.0 * FAR,
                                   bias=neg_top[:, par, 0:1], accum_out=esum[:, par, 0, 0:1])
                    act.activation(scores[:, par, :], scores[:, par, :], ACT.Exp, scale=2.0,
                                   bias=neg_top[:, par, 0:1], accum_out=esum[:, par, 0, 1:2]).then_inc(s_expU, 1)
                    act.wait_ge(s_maxL, s + 1)
                    act.activation(own[:, par, :], own[:, par, :], ACT.Exp, scale=2.0,
                                   bias=neg_top[:, par, 1:2], accum_out=esum[:, par, 1, 1:2])
                    act.activation(adjL[:, :], adjL[:, :], ACT.Exp, scale=2.0 * FAR,
                                   bias=neg_top[:, par, 1:2], accum_out=esum[:, par, 1, 0:1]).then_inc(s_expL, 1)

                def step(s, par):
                    if not (isinstance(s, int) and s == 0):
                        finish_product(s - 1, (s - 1 + HT, s - 1))
                    for c in range(HC):
                        b = (par * (HC + 1) + c) % 2
                        act.wait_ge(s_pT_ps, (HC + 1) * s + c + 1)
                        wait(act, s_pv, (HC + 1) * s + c - 1)
                        act.copy(probT[:, b].rearrange("p j c -> p (j c)"), bank[3 + b][:, :]).then_inc(s_pT, 1)
                    if not (isinstance(s, int) and s == HT - 1):
                        exps(s + 1, 1 - par)

                exps(0, 0)
                pipeline(act, HT, step)
                finish_product(HT - 1, (T - 1, HT - 1))
            with act.Else():
                def pair(s, par):
                    for slot in range(2):
                        n = 2 * s + slot
                        act.wait_ge(g_max, n + 1)
                        act.activation(adjU[:, 0, :], adjU[:, 0, :], ACT.Exp, scale=2.0, bias=neg_top[:, 0, slot:slot + 1],
                                       accum_out=esum[:, 0, slot, 0:1]).then_inc(g_exp, 1)
                        for c in range(NG):
                            act.wait_ge(s_pT_ps, NG * n + c + 1)
                            wait(act, s_pv, NG * n + c - 1)
                            act.copy(probT[:, c % 2].rearrange("p j c -> p (j c)"), bank[3 + c % 2][:, :])\
                               .then_inc(s_pT, 1)
                    finish_product(s, (2 * s, 2 * s + 1))

                pipeline(act, HT, pair)
            act.drain().then_inc(s_var_in, 1)

            done = [0]

            def function(fn, dst, src):
                done[0] += 1
                act.wait_ge(s_f, done[0])
                act.activation(dst[:, :], src[:, :], fn).then_inc(s_fa, 1)

            for fn, i in POINT_FUNCTIONS:
                function(fn, v[i], v[i])
            act.wait_ge(s_f, done[0] + 1)
            with act.Fori(0, HT) as i:
                act.activation(qx[:, 2 * i + 1, 0:D], qx[:, 2 * i + 1, 0:D], ACT.Copy, scale=v[8][:, bass.ds(2 * i + 1, 1)])
            act.drain().then_inc(s_ptsA, 1)

            def mean_tile(t, par):
                for g in range(0, NG, 2):
                    act.wait_ge(d_t_ps, NG * t + g + 1)
                    if g < 4:
                        wait(act, d_mm, NG * t + g - 3)
                    else:
                        act.wait_ge(d_mm, NG * t + g - 3)
                    act.copy(adjT[:, g % 4].rearrange("p j c -> p (j c)"), bank[g % 4][:, :]).then_inc(d_tA, 1)
                    if g == 2 and not (isinstance(t, int) and t == 0):
                        mean_out(t - 1, 1 - par)
                    if g == 6 and not (isinstance(t, int) and t == 0):
                        mean_squares(t - 1, 1 - par)

            def mean_out(t, par):
                act.wait_ge(d_mm, NG * t + NG)
                act.copy(nom[:, par, :], bank[4 + par][:, 0:XW]).then_inc(d_nom, 1)

            def mean_squares(t, par):
                act.wait_ge(d_r, t + 1)
                act.activation(junk[:, 0], nom[:, par, 0:D], ACT.Square, scale=rec[:, par:par + 1],
                               accum_out=sq2[:, 0:1])
                act.activation(junk[:, 1], res[:, t, :], ACT.Square, accum_out=sq2[:, 1:2])
                act.drain()
                act.copy(tm_sq[:, bass.ds(t, 1)], sq2[:, 0:1])
                act.copy(r_sq[:, bass.ds(t, 1)], sq2[:, 1:2])

            pipeline(act, T, mean_tile)
            mean_out(T - 1, 1)
            mean_squares(T - 1, 1)
            act.drain().then_inc(d_sq, 1)
            done[0] += 1
            for fn, i in FINISH_FUNCTIONS:
                function(fn, v[i], v[i])

        @block.vector
        def _(dve):
            dve.memset(ln_eps[:, :], LN_EPS)
            dve.memset(pushed[:, :], PUSHED_OUT)
            for i in range(HT):
                dve.memset(borders[:, i:i + 1], float((i + 1) * P))
            dve.wait_ge(s_ptr, 16)
            dve.tensor_copy(ptr_f[:, :], ptr_i[:, :])
            dve.wait_ge(s_rows, 1)
            dve.tensor_copy(row_no[:, :], row_no_i[:, :])
            dve.wait_ge(s_ident, 3)
            dve.tensor_copy(ident_b[:, :], ident[:, :])
            dve.drain()
            dve.tensor_tensor(counts, row_no[:, :].unsqueeze(2).to_broadcast([P, T, NPTR]),
                              ptr_f[:, :].unsqueeze(1).to_broadcast([P, T, NPTR]), ALU.is_ge)
            dve.drain()
            dve.tensor_reduce(graph_col[:, :], counts, AX.X, ALU.add)
            dve.tensor_tensor(border_eq, borders[:, :].unsqueeze(2).to_broadcast([P, HT, NPTR]),
                              ptr_f[:, :].unsqueeze(1).to_broadcast([P, HT, NPTR]), ALU.is_equal)
            dve.tensor_scalar(in_upper[:, :], ptr_f[:, :], float(HALF), None, ALU.is_gt)
            dve.tensor_scalar(below_end[:, :], ptr_f[:, :], float(N), None, ALU.is_lt)
            dve.drain()
            dve.tensor_reduce(border_hit[:, :], border_eq, AX.X, ALU.max)
            dve.tensor_tensor(in_upper[:, :], in_upper[:, :], below_end[:, :], ALU.mult)
            dve.drain()
            dve.tensor_reduce(checks[:, 0:1], border_hit[:, :], AX.X, ALU.add)
            dve.tensor_reduce(checks[:, 1:2], in_upper[:, :], AX.X, ALU.add)
            dve.drain()
            dve.tensor_tensor(checks[:, 2:3], checks[:, 0:1], checks[:, 1:2], ALU.subtract)
            dve.drain()
            dve.tensor_scalar(fast[:, :], checks[:, 2:3], float(HT), None, ALU.is_ge).then_inc(s_fast, 1)
            for g in range(NG):
                wait(dve, s_grow_ps, g - 1)
                for j in range(BPC):
                    t = g * BPC + j
                    last = dve.tensor_scalar(diag[:, g % 2, j * P:(j + 1) * P], ident_b[:, :],
                                             graph_col[:, t:t + 1], None, ALU.mult)
                last.then_inc(s_diag, 1)
            dve.wait_ge(s_w, 16 * 8)
            dve.tensor_scalar(bqk[:, 0], bqk[:, 0], HALF_SCALE, None, ALU.mult).then_inc(s_const, 1)

            def normalise(g, par):
                if isinstance(g, int):
                    dve.wait_ge(s_xin[par], 16 * (g // 2 + 1))
                else:
                    dve.wait_ge(s_xin[par], g * 8 - 8 * par + 16)
                for j in range(BPC):
                    dve.bn_stats(bnst[:, j, :], xin[:, par, j, :])
                dve.drain()
                for j in range(BPC):
                    last = dve.bn_aggr(mv[:, j, :], bnst[:, j, :])
                last.then_inc(s_var, 1)
                dve.wait_ge(s_std, g + 1)
                dve.reciprocal(rstd[:, :], rstd[:, :])
                dve.drain()
                for j in range(BPC):
                    last = dve.tensor_scalar(xin[:, par, j, :], xin[:, par, j, :], mv[:, j, 0:1], rstd[:, j:j + 1],
                                             ALU.subtract, ALU.mult)
                last.then_inc(s_norm, 1)

            def project(g, par):
                if not (isinstance(g, int) and g == NG - 1):
                    normalise(g + 1, 1 - par)
                for b in range(2):
                    dve.wait_ge(s_v_ps, 2 * g + b + 1)
                    dve.tensor_tensor(val_v[:, g, 2 * b:2 * b + 2, :], bank[6 + b][:, :].rearrange("p (j d) -> p j d", j=2),
                                      bv_row[:, :, :], ALU.add).then_inc(s_v, 1)

            normalise(0, 0)
            pipeline(dve, NG, project)

            def tile_out(groups, s, par, slot, t, one_sum):
                dve.wait_ge(s_pv, groups)
                if one_sum:
                    dve.reciprocal(tot[:, slot:slot + 1], esum[:, par, slot, 0:1])
                else:
                    dve.tensor_tensor(tot[:, slot:slot + 1], esum[:, par, slot, 0:1], esum[:, par, slot, 1:2], ALU.add)
                    dve.drain()
                    dve.reciprocal(tot[:, slot:slot + 1], tot[:, slot:slot + 1])
                dve.drain()
                dve.wait_ge(s_xt[slot], 16 * s + 16)
                wait(dve, s_x1_out[slot], 16 * s)
                dve.scalar_tensor_tensor(out=x1[:, slot], in0=bank[5 + slot][:, 0:D], scalar=tot[:, slot:slot + 1],
                                         in1=xt[:, slot], op0=ALU.mult, op1=ALU.add).then_inc(s_x1, 1)
                dve.drain()
                dve.bn_stats(bn1[:, :], x1[:, slot])
                dve.drain()
                dve.bn_aggr(mv1[:, :], bn1[:, :])
                dve.drain()
                dve.tensor_copy(var_all[:, bass.ds(t, 1)], mv1[:, 1:2])
                dve.tensor_scalar(cent[:, slot], x1[:, slot], mv1[:, 0:1], 0.0, ALU.subtract, ALU.max).then_inc(s_cent, 1)

            dve.wait_ge(s_grow, NG)
            flag = dve.value_load(fast[0:1, 0:1], min_val=0, max_val=1)
            with dve.If(flag > 0):
                def front(s, par):
                    dve.wait_ge(s_adjU[par], 16 * (s // 2) + 16 if isinstance(s, int) else s * 8 - 8 * par + 16)
                    for c in range(HC):
                        cols = slice(HALF + c * CH, HALF + (c + 1) * CH)
                        dve.wait_ge(s_qkU, HC * s + c + 1)
                        dve.sem_inc(s_seen, 1)
                        dve.tensor_tensor_reduce(out=scores[:, par, c * CH:(c + 1) * CH], in0=adjU[:, par, cols],
                                                 in1=bank[1 + c % 2][:, :], scale=1.0, scalar=-3.0e38, op0=ALU.add,
                                                 op1=ALU.max, accum_out=mx[:, c:c + 1]).then_inc(s_qkU_used, 1)
                    dve.tensor_reduce(least[:, :], adjU[:, par, 0:HALF], AX.X, ALU.min)
                    dve.drain()
                    dve.tensor_reduce(top[:, :], mx[:, 0:HC], AX.X, ALU.max)
                    dve.drain()
                    dve.scalar_tensor_tensor(out=top[:, :], in0=least[:, :], scalar=FAR, in1=top[:, :],
                                             op0=ALU.mult, op1=ALU.max)
                    dve.drain()
                    dve.tensor_scalar(neg_top[:, par, 0:1], top[:, :], -2.0, None, ALU.mult).then_inc(s_maxU, 1)
                    dve.wait_ge(s_adjL, 16 * s + 16)
                    dve.tensor_scalar(same[:, par, :], graph_t[:, s, :], graph_col[:, bass.ds(s, 1)], None, ALU.is_equal)
                    dve.drain()
                    dve.tensor_scalar(factor[:, :], same[:, par, :], 1.0 - FAR, FAR, ALU.mult, ALU.add)
                    dve.drain()
                    dve.tensor_tensor(far_part[:, :], adjL_t[:, s, :], factor[:, :], ALU.mult)
                    dve.wait_ge(s_qkL, s + 1)
                    dve.tensor_tensor(near_part[:, :], same[:, par, :], bank[0][:, 0:P], ALU.mult).then_inc(s_qkL_used, 1)
                    dve.drain()
                    dve.tensor_copy(adjL_t[:, s, :], pushed[:, :])
                    dve.drain()
                    dve.tensor_tensor_reduce(out=own[:, par, :], in0=far_part[:, :], in1=near_part[:, :], scale=1.0,
                                             scalar=-3.0e38, op0=ALU.add, op1=ALU.max, accum_out=top[:, :])
                    dve.tensor_reduce(least[:, :], adjL[:, :], AX.X, ALU.min)
                    dve.drain()
                    dve.scalar_tensor_tensor(out=top[:, :], in0=least[:, :], scalar=FAR, in1=top[:, :],
                                             op0=ALU.mult, op1=ALU.max)
                    dve.drain()
                    dve.tensor_scalar(neg_top[:, par, 1:2], top[:, :], -2.0, None, ALU.mult).then_inc(s_maxL, 1)

                def step(s, par):
                    if not (isinstance(s, int) and s == HT - 1):
                        front(s + 1, 1 - par)
                    b = (par * (HC + 1) + HC) % 2
                    dve.wait_ge(s_pT_ps, (HC + 1) * s + HC + 1)
                    dve.wait_ge(s_pv, (HC + 1) * s + HC - 1)
                    dve.tensor_tensor(probT[:, b, 0, :], same[:, par, :], bank[3 + b][:, 0:P], ALU.mult).then_inc(s_pTL, 1)
                    tile_out((HC + 1) * s + HC, s, par, 0, s + HT, False)
                    tile_out((HC + 1) * s + HC + 1, s, par, 1, s, False)

                front(0, 0)
                pipeline(dve, HT, step)
            with dve.Else():
                def pair(s, par):
                    for slot in range(2):
                        n = 2 * s + slot
                        dve.wait_ge(g_adj, 16 * n + 16)
                        for c in range(NG):
                            cols = slice(c * CH, (c + 1) * CH)
                            dve.tensor_scalar(mask_c, graph_row[:, cols], graph_col[:, bass.ds(n, 1)], None, ALU.is_equal)
                            dve.drain()
                            dve.tensor_scalar(factor_c, mask_c, 1.0 - FAR, FAR, ALU.mult, ALU.add)
                            dve.wait_ge(g_qk, NG * n + c + 1)
                            dve.tensor_tensor(near_c, mask_c, bank[1 + c % 2][:, :], ALU.mult).then_inc(g_qk_used, 1)
                            dve.drain()
                            dve.tensor_tensor(adjU[:, 0, cols], adjU[:, 0, cols], factor_c, ALU.mult)
                            dve.drain()
                            dve.tensor_tensor_reduce(out=adjU[:, 0, cols], in0=adjU[:, 0, cols], in1=near_c, scale=1.0,
                                                     scalar=-3.0e38, op0=ALU.add, op1=ALU.max, accum_out=mx[:, c:c + 1])
                            dve.drain()
                        dve.tensor_reduce(top[:, :], mx[:, 0:NG], AX.X, ALU.max)
                        dve.drain()
                        dve.tensor_scalar(neg_top[:, 0, slot:slot + 1], top[:, :], -2.0, None, ALU.mult).then_inc(g_max, 1)
                        dve.wait_ge(g_exp, n + 1)
                        for c in range(NG):
                            cols = slice(c * CH, (c + 1) * CH)
                            dve.tensor_scalar(mask_c, graph_row[:, cols], graph_col[:, bass.ds(n, 1)], None, ALU.is_equal)
                            dve.drain()
                            dve.tensor_tensor(adjU[:, 0, cols], adjU[:, 0, cols], mask_c, ALU.mult)
                            dve.drain()
                        dve.drain().then_inc(g_mask, 1)
                        tile_out(NG * n + NG, s, 0, slot, n, True)

                pipeline(dve, HT, pair)

            asked = [0]
            taken = [0]

            def function(last):
                last.then_inc(s_f, 1)
                asked[0] += 1
                dve.wait_ge(s_fa, asked[0])

            def ts(o, a, s1, s2, op0, op1=ALU.bypass):
                last = dve.tensor_scalar(o, a, s1, s2, op0, op1) if s2 is not None else dve.tensor_scalar(o, a, s1, None, op0)
                return last

            def tt(o, a, b, op):
                return dve.tensor_tensor(o, a, b, op)

            def artanh(o, a, t1, t2, t3, fn):
                ts(t1, a, -1.0, 1.0, ALU.mult, ALU.add)
                ts(t2, a, 1.0, None, ALU.add)
                dve.drain()
                dve.reciprocal(t1, t1)
                dve.drain()
                fn(tt(t1, t1, t2, ALU.mult))
                tt(t2, a, a, ALU.mult)
                dve.drain()
                ts(t3, t2, 1.0 / 13, 1.0 / 11, ALU.mult, ALU.add)
                for c in (9, 7, 5, 3, 1):
                    dve.drain()
                    tt(t3, t3, t2, ALU.mult)
                    dve.drain()
                    ts(t3, t3, 1.0 / c, None, ALU.add)
                dve.drain()
                tt(t3, t3, a, ALU.mult)
                ts(t1, t1, 0.5, None, ALU.mult)
                ts(t2, a, TINY_ARG, None, ALU.is_lt)
                dve.drain()
                tt(t3, t3, t1, ALU.subtract)
                dve.drain()
                tt(t3, t3, t2, ALU.mult)
                dve.drain()
                tt(o, t1, t3, ALU.add)
                dve.drain()

            V = [a[:, :] for a in v]
            dve.drain()
            dve.wait_ge(s_var_in, 1)
            function(ts(V[0], var_all[:, :], LN_EPS, None, ALU.add))
            dve.reciprocal(V[0], V[0])
            dve.drain()
            tt(V[3], V[0], V[0], ALU.mult)
            dve.drain()
            tt(V[1], V[3], cent_sq[:, :], ALU.mult)
            tt(V[4], V[3], mx_sq[:, :], ALU.mult)
            dve.drain()
            function(ts(V[1], V[1], FLOOR, None, ALU.max))
            function(ts(V[2], V[4], FLOOR, None, ALU.max))
            ts(V[3], V[1], CLIP, None, ALU.min)
            dve.drain()
            artanh(V[3], V[3], V[5], V[6], V[7], function)
            dve.reciprocal(V[1], V[1])
            tt(V[3], V[3], V[2], ALU.mult)
            dve.drain()
            function(tt(V[3], V[3], V[1], ALU.mult))
            dve.reciprocal(V[2], V[2])
            ts(V[4], V[4], FLOOR, None, ALU.is_gt)
            dve.drain()
            tt(V[3], V[3], V[2], ALU.mult)
            tt(V[4], V[4], V[0], ALU.mult)
            dve.drain()
            tt(V[3], V[3], V[4], ALU.mult)
            dve.drain()
            tt(V[4], V[3], V[3], ALU.mult)
            dve.drain()
            tt(V[4], V[4], mx_sq[:, :], ALU.mult)
            dve.drain()
            ts(V[4], V[4], -1.0, 1.0, ALU.mult, ALU.add)
            dve.drain()
            dve.reciprocal(V[4], V[4])
            dve.drain()
            ts(V[4], V[4], 2.0, 1e-15, ALU.mult, ALU.max)
            dve.drain()
            tt(V[8], V[3], V[4], ALU.mult).then_inc(s_f, 1)
            ts(qx[:, :, D:D + 1].rearrange("p t a -> p (t a)"), V[4], -1.0, None, ALU.add)
            dve.memset(qx[:, :, D + 1:D + 2].rearrange("p t a -> p (t a)"), 1.0)
            dve.drain()
            with dve.Fori(0, HT) as i:
                dve.tensor_scalar(qx[:, 2 * i, 0:D], qx[:, 2 * i, 0:D], v[8][:, bass.ds(2 * i, 1)], None, ALU.mult)
            dve.drain().then_inc(s_pts, 1)

            def mean_tile(t, par):
                for g in range(1, NG, 2):
                    dve.wait_ge(d_t_ps, NG * t + g + 1)
                    wait(dve, d_mm, NG * t + g - 3)
                    dve.tensor_copy(adjT[:, g % 4].rearrange("p j c -> p (j c)"), bank[g % 4][:, :]).then_inc(d_tV, 1)
                    if g == 5 and not (isinstance(t, int) and t == 0):
                        mean_relu(t - 1, 1 - par)

            def mean_relu(t, par):
                dve.wait_ge(d_nom, t + 2)
                ts(sgn[:, :], nom[:, par, D:D + 2], 0.0, 2.0, ALU.is_ge, ALU.mult)
                dve.drain()
                ts(sgn[:, :], sgn[:, :], -1.0, None, ALU.add)
                dve.drain()
                tt(size[:, :], nom[:, par, D:D + 2], sgn[:, :], ALU.mult)
                dve.drain()
                ts(rec[:, par:par + 1], size[:, 0:1], EPS, None, ALU.max)
                dve.tensor_copy(alpha[:, bass.ds(t, 1)], size[:, 1:2])
                dve.drain()
                dve.reciprocal(rec[:, par:par + 1], rec[:, par:par + 1])
                dve.drain()
                dve.scalar_tensor_tensor(out=turn[:, 0:1], in0=sgn[:, 0:1], scalar=sgn[:, 1:2],
                                         in1=rec[:, par:par + 1], op0=ALU.mult, op1=ALU.mult)
                dve.drain()
                ts(res[:, t, :], nom[:, par, 0:D], turn[:, 0:1], 0.0, ALU.mult, ALU.max).then_inc(d_r, 1)

            pipeline(dve, T, mean_tile)
            mean_relu(T - 1, 1)

            dve.drain()
            dve.wait_ge(d_sq, 1)
            ts(V[0], tm_sq[:, :], -1.0, 1.0, ALU.mult, ALU.add)
            dve.drain()
            function(ts(V[0], V[0], EPS, None, ALU.max))
            ts(V[0], V[0], 1.0, None, ALU.add)
            dve.drain()
            dve.reciprocal(V[0], V[0])
            dve.drain()
            tt(V[1], V[0], V[0], ALU.mult)
            dve.drain()
            tt(V[1], V[1], tm_sq[:, :], ALU.mult)
            dve.drain()
            function(ts(V[1], V[1], FLOOR, None, ALU.max))
            ts(V[2], V[1], CLIP, None, ALU.min)
            dve.drain()
            artanh(V[2], V[2], V[5], V[6], V[7], function)
            function(tt(V[2], V[2], alpha[:, :], ALU.mult))
            dve.reciprocal(V[1], V[1])
            tt(V[0], V[0], V[2], ALU.mult)
            dve.drain()
            tt(V[0], V[0], V[1], ALU.mult)
            dve.drain()
            tt(V[1], V[0], V[0], ALU.mult)
            dve.drain()
            tt(V[1], V[1], tm_sq[:, :], ALU.mult)
            dve.drain()
            function(ts(V[1], V[1], FLOOR, None, ALU.max))
            ts(V[2], V[1], CLIP, None, ALU.min)
            dve.drain()
            artanh(V[2], V[2], V[5], V[6], V[7], function)
            dve.reciprocal(V[1], V[1])
            tt(V[0], V[0], V[2], ALU.mult)
            dve.drain()
            tt(V[0], V[0], V[1], ALU.mult)
            dve.drain()
            tt(V[1], V[0], V[0], ALU.mult)
            dve.drain()
            tt(V[1], V[1], r_sq[:, :], ALU.mult)
            dve.drain()
            function(ts(V[1], V[1], FLOOR, None, ALU.max))
            dve.reciprocal(V[3], V[1])
            dve.drain()
            function(tt(V[1], V[1], V[1], ALU.max))
            tt(V[0], V[0], V[3], ALU.mult)
            dve.drain()
            tt(V[0], V[0], V[1], ALU.mult)
            dve.drain()
            dve.wait_ge(s_x1_all, 16 * (NG // 4))
            for g in range(NG):
                for j in range(BPC):
                    t = g * BPC + j
                    last = dve.scalar_tensor_tensor(out=res[:, t, :], in0=res[:, t, :], scalar=v[0][:, t:t + 1],
                                                    in1=x1_all[:, t, :], op0=ALU.mult, op1=ALU.add)
                last.then_inc(s_out, 1)


_INS = ["x", "adj", "L0_gnn_ptr", "L0_gnn_Wq", "L0_gnn_bq", "L0_gnn_Wk", "L0_gnn_bk", "L0_gnn_Wv", "L0_gnn_bv",
        "L1_gnn_W"]


def kernel(**inputs):
    import numpy as _np
    import concourse.bacc as _bacc
    from concourse import mybir as _mybir
    from concourse.bass_utils import run_bass_kernel_spmd as _run

    nc = _bacc.Bacc("TRN2", target_bir_lowering=False, num_devices=1, dynamic_dma_scratch_size=1024)
    arrays, args = {}, []
    for name in _INS:
        a = _np.ascontiguousarray(inputs[name])
        arrays[f"in_{name}"] = a
        args.append(nc.dram_tensor(f"in_{name}", a.shape, _mybir.dt.from_np(a.dtype), kind="ExternalInput").ap())
    shape = inputs["x"].shape
    args.append(nc.dram_tensor("out_x", shape, _mybir.dt.float32, kind="ExternalOutput").ap())
    graph_layers_kernel(nc, *args)
    r = _run(nc, [arrays], core_ids=[0])
    return r.results[0]["out_x"]
```

```python
import concourse.bass as bass
from concourse import mybir
from contextlib import ExitStack

F32 = mybir.dt.float32
BF16 = mybir.dt.bfloat16
F32R = mybir.dt.float32r
I32 = mybir.dt.int32
ALU = mybir.AluOpType
ACT = mybir.ActivationFunctionType
AX = mybir.AxisListType

P = 128
LN_EPS = 1e-5
FAR = -1.0e6
FLOOR = 1e-20
EPS = 1e-10
CLIP = 1.0 - 1e-7
TINY_ARG = 0.25
PUSHED_OUT = 1.0e30


UPPER_BANK = (5, 0)

POINT_FUNCTIONS = [(ACT.Sqrt, 0), (ACT.Sqrt, 1), (ACT.Sqrt, 2), (ACT.Ln, 5), (ACT.Tanh, 3)]
FINISH_FUNCTIONS = [(ACT.Sqrt, 0), (ACT.Sqrt, 1), (ACT.Ln, 5), (ACT.Tanh, 2), (ACT.Sqrt, 1), (ACT.Ln, 5),
                    (ACT.Sqrt, 1), (ACT.Tanh, 1)]


def graph_layers_kernel(nc, x, adj, ptr, Wq, bq, Wk, bk, Wv, bv, W, out):
    N, D = x.shape
    T = N // P
    HT = T // 2
    KD = D // P
    CH = 512
    BPC = CH // P
    NG = N // CH
    HALF = N // 2
    HC = HALF // CH
    NPTR = ptr.shape[0]
    XW = D + 2
    HALF_SCALE = 0.5 / float(D) ** 0.5

    x_g = x.rearrange("(g j p) d -> g p j d", p=P, j=BPC)
    x_halves = x.rearrange("(h s p) d -> s p h d", p=P, h=2)
    x_pairs = x.rearrange("(s h p) d -> s p h d", p=P, h=2)
    adj_t = adj.rearrange("(t p) n -> t p n", p=P)
    out_g = out.rearrange("(g j p) d -> g p j d", p=P, j=BPC)

    ctx = ExitStack()
    with ctx:
        def sb(name, shape, dt=F32):
            return ctx.enter_context(nc.sbuf_tensor(name, shape, dt))

        def sem(name):
            return ctx.enter_context(nc.semaphore(name))

        x1_dram = nc.dram_tensor("x1_scratch", [N, D], F32, kind="Internal").ap()
        x1_halves = x1_dram.rearrange("(h s p) d -> s p h d", p=P, h=2)
        x1_pairs = x1_dram.rearrange("(s h p) d -> s p h d", p=P, h=2)

        w1 = sb("w1", [P, KD, D])
        bqk = sb("bqk", [P, 2, KD])
        bv_row = sb("bv_row", [P, 2, D])
        junk = sb("junk", [P, 4, D], BF16)
        ident = sb("ident", [P, P])
        ident_b = sb("ident_b", [P, P], BF16)
        ones_b = sb("ones_b", [P, P], BF16)
        diag = sb("diag", [P, 2, CH], BF16)
        graph_col = sb("graph_col", [P, T])
        row_no = sb("row_no", [P, T])
        row_no_i = sb("row_no_i", [P, T], I32)
        ptr_i = sb("ptr_i", [P, NPTR], I32)
        ptr_f = sb("ptr_f", [P, NPTR])
        in_upper = sb("in_upper", [P, NPTR])
        below_end = sb("below_end", [P, NPTR])
        borders = sb("borders", [P, HT])
        border_hit = sb("border_hit", [P, HT])
        checks = sb("checks", [P, 4])
        fast = sb("fast", [P, 1], I32)
        ln_eps = sb("ln_eps", [P, 1])
        bnst = sb("bnst", [P, BPC, 6])
        mv = sb("mv", [P, BPC, 2])
        rstd = sb("rstd", [P, BPC])
        mx = sb("mx", [P, 8])
        top = sb("top", [P, 1])
        least = sb("least", [P, 1])
        neg_top = sb("neg_top", [P, 2, 2])
        esum = sb("esum", [P, 2, 2, 2])
        tot = sb("tot", [P, 2])
        bn1 = sb("bn1", [P, 6])
        mv1 = sb("mv1", [P, 2])
        var_all = sb("var_all", [P, T])
        cent_sq = sb("cent_sq", [P, T])
        mx_sq = sb("mx_sq", [P, T])
        sq2 = sb("sq2", [P, 4])
        tm_sq = sb("tm_sq", [P, T])
        r_sq = sb("r_sq", [P, T])
        alpha = sb("alpha", [P, T])
        v = [sb(f"v{i}", [P, T]) for i in range(9)]
        rec = sb("rec", [P, 2])
        sgn = sb("sgn", [P, 2])
        size = sb("size", [P, 2])
        turn = sb("turn", [P, 2])

        region, at = {}, -(-nc.sbuf_base // 32) * 32
        for name, size_b in (("keys", 3 * KD * HALF * 4), ("values", T * D * 4), ("qx", T * XW * 4),
                             ("graph", N * 2), ("adjL", 2 * N * 4), ("scores", 2 * HALF * 4),
                             ("adjU", N * 4), ("small", 46 * P * 4)):
            region[name] = at
            at += -(-size_b // 32) * 32

        def place(name, shape, where, offset=0, dt=F32):
            return nc.alloc_sbuf_tensor_at(name, shape, dt, offset=region[where] + offset)

        values = place("values", [P, T, D], "values")
        qx = place("qx", [P, T, XW], "qx")
        graph_row = place("graph_row", [P, N], "graph", dt=BF16)
        xin = place("xin", [P, 2, BPC, D], "adjL", N * 4)
        w_raw = place("w_raw", [P, 3, KD, D], "scores")
        counts = place("counts", [P, T, NPTR], "adjU")
        border_eq = place("border_eq", [P, HT, NPTR], "adjL")
        small = iter(range(0, 46 * P * 4, P * 4))

        def place_small(name, shape, dt=F32):
            words = 1
            for n in shape[1:]:
                words *= n
            first = next(small)
            for _ in range(words // P - 1):
                next(small)
            return place(name, shape, "small", first, dt)

        probT = place_small("probT", [P, 2, BPC, P])
        xt = place_small("xt", [P, 2, 2, D])
        x1 = place_small("x1", [P, 2, D])
        cent = place_small("cent", [P, 2, D])
        centT = place_small("centT", [P, 2, KD, P])
        own = place_small("own", [P, 2, P])
        same = place_small("same", [P, 2, P])
        factor = place_small("factor", [P, P])
        far_part = place_small("far_part", [P, P])
        near_part = place_small("near_part", [P, P])
        pushed = place_small("pushed", [P, P])
        q_low = place_small("q_low", [P, KD, P])
        stage_at = next(small)
        q_hi = place("q_hi", [P, KD, P], "small", stage_at, F32R)
        q_lo = place("q_lo", [P, KD, P], "small", stage_at + KD * P * 4, F32R)
        keysU_hi = place("keysU_hi", [P, KD, HALF], "keys", 0, F32R)
        keysU_lo = place("keysU_lo", [P, KD, HALF], "keys", KD * HALF * 4, F32R)
        keysL = place("keysL", [P, KD, HALF], "keys", 2 * KD * HALF * 4)
        hT_hi = place("hT_hi", [P, 2, KD, CH], "scores", 0, F32R)
        hT_lo = place("hT_lo", [P, 2, KD, CH], "scores", 2 * KD * CH * 4, F32R)
        wT_hi = place("wT_hi", [P, 3, KD, D], "adjL", N * 4 + 2 * BPC * D * 4, F32R)
        wT_lo = place("wT_lo", [P, 3, KD, D], "small", 0, F32R)
        adjL = place("adjL", [P, 2, N], "adjL")
        adjU = place("adjU", [P, N], "adjU")
        scores = place("scores", [P, 2, HALF], "scores")
        mask_c = place("mask_c", [P, CH], "scores")
        factor_c = place("factor_c", [P, CH], "scores", CH * 4)
        near_c = place("near_c", [P, CH], "scores", 2 * CH * 4)
        X_hi = place("X_hi", [P, T, XW], "keys", 0, F32R)
        X_lo = place("X_lo", [P, T, XW], "keys", T * XW * 4, F32R)
        adjT_hi = place("adjT_hi", [P, 4, BPC, P], "keys", 2 * T * XW * 4, F32R)
        adjT_lo = place("adjT_lo", [P, 4, BPC, P], "scores", 0, F32R)
        nom = place("nom", [P, 2, XW], "scores", 4 * BPC * P * 4)
        res = place("res", [P, T, D], "adjU")
        x1_all = place("x1_all", [P, T, D], "qx")

        qx_v = qx[:, :, :].rearrange("p (g j) c -> p g j c", j=BPC)
        qx_halves = qx[:, :, :].rearrange("p (h s) c -> p h s c", h=2)
        qx_pairs = qx[:, :, :].rearrange("p (s h) c -> p h s c", h=2)
        val_v = values[:, :, :].rearrange("p (g j) d -> p g j d", j=BPC)
        keysL_t = keysL[:, :, :].rearrange("p k (t c) -> p k t c", c=P)
        graph_t = graph_row[:, :].rearrange("p (t c) -> p t c", c=P)
        adjL_t = adjL[:, :, :].rearrange("p a (t c) -> p a t c", c=P)

        bank = [ctx.enter_context(nc.psum_tensor(f"bank{i}", [P, CH], F32)) for i in range(8)]

        s_ptr = sem("ptr_in")
        s_w = sem("weights_in")
        s_xin = [sem("x_group_in0"), sem("x_group_in1")]
        s_ident = sem("ident_ready")
        s_rows = sem("row_numbers_ready")
        s_const = sem("vector_constants_ready")
        s_setup = sem("vector_setup_steps")
        s_wt_ps = sem("weights_turned")
        s_wt_hi = sem("turned_weights_high_ready")
        s_wt = sem("turned_weights_ready")
        s_diag = sem("diag_ready")
        s_grow_ps = sem("graph_row_in_psum")
        s_grow = sem("graph_row_copied")
        s_fast = sem("path_chosen")
        s_var = sem("variance_ready")
        s_std = sem("deviation_ready")
        s_norm = sem("normalised")
        s_hT_ps = sem("h_turned")
        s_hT_hi = sem("hT_high_ready")
        s_hT = sem("hT_ready")
        s_kq_ps = sem("keys_queries_in_psum")
        s_kq = sem("keys_queries_copied")
        s_key_lo = sem("upper_keys_low_ready")
        s_v_ps = sem("values_in_psum")
        s_v = sem("values_copied")
        s_window = sem("adj_upper_window_in")
        s_beside = sem("adj_upper_rest_in")
        s_adjL = [sem("adj_lower_in0"), sem("adj_lower_in1")]
        s_xt = [sem("x_pair_in0"), sem("x_pair_in1")]
        s_x1_out = sem("x1_stored")
        s_q = sem("queries_staged")
        s_qk = sem("scores_in_psum")
        s_qk_used = sem("scores_read")
        s_seen = sem("waits_carried_for_reduces")
        s_sync_seen = sem("waits_carried_for_addresses")
        s_maxU = sem("upper_maximum_ready")
        s_maxL = sem("lower_maximum_ready")
        s_expU = sem("upper_exp_done")
        s_own = sem("own_exp_done")
        s_own_m = sem("own_exp_masked")
        s_expL = sem("lower_exp_done")
        s_pT_ps = sem("exp_turned")
        s_pT = sem("turned_exp_copied")
        s_pv = sem("group_of_values_summed")
        s_x1 = sem("x1_ready")
        s_cent = sem("centred_ready")
        s_csq = sem("centred_squared")
        s_cT_ps = sem("centred_turned")
        s_cT = sem("centred_copied")
        s_mx_ps = sem("product_in_psum")
        s_mx = sem("product_copied")
        g_adj = sem("general_adj_in")
        g_qk = sem("general_scores_in_psum")
        g_qk_used = sem("general_scores_read")
        g_max = sem("general_maximum_ready")
        g_exp = sem("general_exp_done")
        g_mask = sem("general_exp_masked")
        s_var_in = sem("statistics_complete")
        s_f = sem("factor_step")
        s_fa = sem("factor_function")
        s_edge = sem("last_columns_ready")
        s_hi = sem("points_high_ready")
        s_lo = sem("points_low_ready")
        d_adj = [sem("mean_adj_in0"), sem("mean_adj_in1")]
        d_t_ps = sem("adj_turned")
        d_hi = sem("turned_adj_high_ready")
        d_lo = sem("turned_adj_low_ready")
        d_mm = sem("group_of_mean_summed")
        d_nom = sem("mean_copied")
        d_r = sem("mean_relu_ready")
        d_sq = sem("mean_squares_ready")
        s_x1_all = sem("x1_back")
        s_out = sem("out_group_ready")
        s_stored = sem("out_stored")

        def wait(eng, s, value):
            if not isinstance(value, int) or value > 0:
                eng.wait_ge(s, value)

        def always(eng):
            eng.wait_ge(s_ident, 3)

        def pipeline(eng, n, step, peel=1):
            for s in range(peel):
                step(s, s % 2)
            with eng.Fori(0, (n - 2 * peel) // 2) as i:
                step(2 * i + peel, peel % 2)
                step(2 * i + peel + 1, 1 - peel % 2)
            for s in range(n - peel, n):
                step(s, s % 2)

        def is_step(s, value):
            return isinstance(s, int) and s == value

        def after(s, value):
            return not isinstance(s, int) or s > value

        def turns(s, par):
            return 16 * ((s - par) // 2 + 1) if isinstance(s, int) else s * 8 - 8 * par + 16

        block = ctx.enter_context(nc.Block())

        @block.sync
        def _(sp):
            sp.dma_start(ptr_i[:, :], ptr.rearrange("(a k) -> a k", a=1).partition_broadcast(P)).then_inc(s_ptr, 16)
            sp.dma_start(xin[:, 0], x_g[0]).then_inc(s_xin[0], 16)
            for n, w in enumerate((Wq, Wk, Wv)):
                sp.dma_start(w_raw[:, n], w.rearrange("(h p) d -> p h d", p=P)).then_inc(s_w, 16)
            with nc.allow_non_contiguous_dma(reason="biases, one column each"):
                sp.dma_start(bqk[:, 0], bq.rearrange("(h p) -> p h", p=P)).then_inc(s_w, 16)
                sp.dma_start(bqk[:, 1], bk.rearrange("(h p) -> p h", p=P)).then_inc(s_w, 16)
            for j in range(2):
                sp.dma_start(bv_row[:, j], bv.rearrange("(a d) -> a d", a=1).partition_broadcast(P)).then_inc(s_w, 16)
            sp.dma_start(w1[:, :, :], W.rearrange("(k p) d -> p k d", p=P)).then_inc(s_w, 16)
            sp.dma_start(xin[:, 1], x_g[1]).then_inc(s_xin[1], 16)

            def x_group(g, par):
                sp.wait_ge(s_hT_ps, g - 1)
                sp.dma_start(xin[:, par], x_g[g]).then_inc(s_xin[par], 16)

            with sp.Fori(0, (NG - 2) // 2) as i:
                x_group(2 * i + 2, 0)
                x_group(2 * i + 3, 1)

            def x_pair(s, par, view):
                wait(sp, s_x1, 2 * s - 2)
                sp.dma_start(xt[:, par], view[s]).then_inc(s_xt[par], 16)

            def x1_store(s, view):
                sp.wait_ge(s_x1, 2 * s + 2)
                sp.dma_start(view[s], x1[:, :, :]).then_inc(s_x1_out, 16)

            def mean_adj(t):
                sp.dma_start(adjL[:, t % 2], adj_t[t]).then_inc(d_adj[t % 2], 16)

            sp.wait_ge(s_fast, 1)
            flag = sp.value_load(fast[0:1, 0:1], min_val=0, max_val=1)
            with sp.If(flag > 0):
                sp.dma_start(adjU[:, HALF:N], adj_t[HT][:, HALF:N]).then_inc(s_window, 16)
                sp.dma_start(adjU[:, 0:HALF], adj_t[HT][:, 0:HALF]).then_inc(s_beside, 16)
                sp.dma_start(adjL[:, 0], adj_t[0]).then_inc(s_adjL[0], 16)
                sp.wait_ge(s_v_ps, 2 * NG)

                def step(s, par):
                    if not is_step(s, HT - 1):
                        sp.wait_ge(s_qk_used, (HC + 1) * s + HC)
                        sp.dma_start(adjU[:, HALF:N], adj_t[s + HT + 1][:, HALF:N]).then_inc(s_window, 16)
                        wait(sp, s_expL, s)
                        sp.dma_start(adjL[:, 1 - par], adj_t[s + 1]).then_inc(s_adjL[1 - par], 16)
                    if after(s, 1):
                        x1_store(s - 2, x1_halves)
                    x_pair(s, par, x_halves)
                    if not is_step(s, HT - 1):
                        sp.wait_ge(s_expU, s + 1)
                        sp.sem_inc(s_sync_seen, 1)
                        sp.dma_start(adjU[:, 0:HALF], adj_t[s + HT + 1][:, 0:HALF]).then_inc(s_beside, 16)

                pipeline(sp, HT, step, 2)
                x1_store(HT - 2, x1_halves)
                sp.wait_ge(s_expL, HT)
                mean_adj(0)
                mean_adj(1)
                x1_store(HT - 1, x1_halves)
            with sp.Else():
                sp.wait_ge(s_v_ps, 2 * NG)

                def pair(s, par):
                    x_pair(s, par, x_pairs)
                    for slot in range(2):
                        n = 2 * s + slot
                        wait(sp, s_pT_ps, n * NG)
                        sp.dma_start(adjL[:, 0], adj_t[n]).then_inc(g_adj, 16)
                    x1_store(s, x1_pairs)

                pipeline(sp, HT, pair, 2)
                sp.wait_ge(s_mx, HT)
                mean_adj(0)
                mean_adj(1)

            sp.wait_ge(s_x1_out, 16 * HT)
            sp.wait_ge(s_lo, T)
            def mean_adj_next(t, par):
                sp.wait_ge(d_t_ps, NG * t + NG)
                sp.dma_start(adjL[:, par], adj_t[t + 2]).then_inc(d_adj[par], 16)

            for t in range(4):
                mean_adj_next(t, t % 2)
                sp.dma_start(x1_all[:, t * HT // 2:(t + 1) * HT // 2, :],
                             x1_dram[t * N // 4:(t + 1) * N // 4, :].rearrange("(t p) d -> p t d", p=P))\
                  .then_inc(s_x1_all, 16)
            with sp.Fori(2, HT - 1) as i:
                for par in range(2):
                    mean_adj_next(2 * i + par, par)
            for g in range(NG):
                sp.wait_ge(s_out, g + 1)
                sp.dma_start(out_g[g], res[:, g * BPC:(g + 1) * BPC, :]).then_inc(s_stored, 16)
            sp.wait_ge(s_stored, 16 * NG)

        @block.gpsimd
        def _(pool):
            pool.iota(row_no_i[:, :], pattern=[[P, T]], base=0, channel_multiplier=1).then_inc(s_rows, 1)
            pool.memset(ident[:, :], 0.0).then_inc(s_ident, 1)
            pool.memset(ones_b[:, :], 1.0).then_inc(s_ident, 1)
            pool.wait_ge(s_ident, 2)
            pool.affine_select(out=ident[:, :], in_=ident[:, :], compare_op=ALU.not_equal, fill=1.0, base=0,
                               pattern=[[-1, P]], channel_multiplier=1).then_inc(s_ident, 1)

            pool.wait_ge(s_kq, 2 * KD * NG)
            pool.wait_ge(s_fast, 1)
            flag = pool.value_load(fast[0:1, 0:1], min_val=0, max_val=1)
            def stage(t):
                always(pool)
                pool.tensor_copy(q_hi[:, :, :].rearrange("p k c -> p (k c)"), qx[:, t, 0:D])
                pool.drain()
                pool.tensor_tensor(q_lo[:, :, :].rearrange("p k c -> p (k c)"), qx[:, t, 0:D],
                                   q_hi[:, :, :].rearrange("p k c -> p (k c)").bitcast(F32), ALU.subtract)\
                    .then_inc(s_q, 1)

            def stage_low(t):
                always(pool)
                pool.tensor_copy(q_low[:, :, :].rearrange("p k c -> p (k c)"), qx[:, t, 0:D]).then_inc(s_q, 1)

            with pool.If(flag > 0):
                def stage_pair(s):
                    wait(pool, s_qk, (HC + 1) * s)
                    stage(s + HT)
                    stage_low(s)

                def step(s, par):
                    if not is_step(s, HT - 1):
                        stage_pair(s + 1)
                    pool.wait_ge(s_own, s + 1)
                    always(pool)
                    pool.tensor_tensor(own[:, par, :], own[:, par, :], same[:, par, :], ALU.mult).then_inc(s_own_m, 1)

                stage_pair(0)
                pipeline(pool, HT, step)
            with pool.Else():
                def pair(s, par):
                    for slot in range(2):
                        n = 2 * s + slot
                        wait(pool, g_qk, NG * n)
                        stage(n)
                        stage_low(n)

                pipeline(pool, HT, pair)

        @block.tensor
        def _(pe):
            pe.wait_ge(s_ident, 3)
            pe.wait_ge(s_w, 16 * 8)
            for n in range(3):
                for h in range(KD):
                    for k in range(KD):
                        last = pe.transpose(bank[n][:, k * D + h * P:k * D + (h + 1) * P],
                                            w_raw[:, n, h, k * P:(k + 1) * P], ident[:, :])
                last.then_inc(s_wt_ps, 1)
            for g in range(NG):
                pe.wait_ge(s_diag, g + 1)
                wait(pe, s_grow, g - 1)
                pe.matmul(bank[3 + g % 2][:, :], ones_b[:, :], diag[:, g % 2, :], start=True, stop=True)\
                  .then_inc(s_grow_ps, 1)

            def turn_h(g, par):
                pe.wait_ge(s_norm, g + 1)
                wait(pe, s_hT, KD * g)
                for k in range(KD):
                    for j in range(BPC):
                        last = pe.transpose(bank[k][:, j * P:(j + 1) * P], xin[:, par, j, k * P:(k + 1) * P],
                                            ident[:, :])
                last.then_inc(s_hT_ps, 1)

            def three(dst, a, b, a_cols, b_cols, k_first=True, k_last=True):
                for n, (i, j) in enumerate(((0, 0), (0, 1), (1, 0))):
                    last = pe.matmul(dst, a[i][a_cols], b[j][b_cols], start=(k_first and n == 0),
                                     stop=(k_last and n == 2))
                return last

            hT_parts, wT_parts = (hT_hi, hT_lo), (wT_hi, wT_lo)
            every = slice(None)

            def project(g, par):
                pe.wait_ge(s_hT, KD * (g + 1))
                for w in range(2):
                    for h in range(KD):
                        i = w * KD + h
                        wait(pe, s_kq, 4 * g + i - 3)
                        if w == 1 and g > NG // 2:
                            pe.wait_ge(s_key_lo, KD * (g - NG // 2 - 1) + h + 1)
                        for k in range(KD):
                            last = three(bank[2 + i][:, :], wT_parts, hT_parts,
                                         (every, w, k, slice(h * P, (h + 1) * P)), (every, par, k, every),
                                         k == 0, k == KD - 1)
                        last.then_inc(s_kq_ps, 1)

                if g < NG - 1:
                    turn_h(g + 1, 1 - par)
                for b in range(2):
                    wait(pe, s_v, 2 * g + b - 1)
                    for j in range(2):
                        for k in range(KD):
                            last = three(bank[6 + b][:, j * D:(j + 1) * D], hT_parts, wT_parts,
                                         (every, par, k, slice((2 * b + j) * P, (2 * b + j + 1) * P)),
                                         (every, 2, k, every), k == 0, k == KD - 1)
                    last.then_inc(s_v_ps, 1)

            pe.wait_ge(s_grow, NG)
            pe.wait_ge(s_wt, 3)
            turn_h(0, 0)
            for g in range(NG):
                project(g, g % 2)
            pe.wait_ge(s_kq, 4 * NG)
            pe.wait_ge(s_key_lo, KD * NG // 2)
            pe.wait_ge(s_v, 2 * NG)
            q_parts, keysU_parts = (q_hi, q_lo), (keysU_hi, keysU_lo)

            def turn_cent(s):
                pe.wait_ge(s_cent, 2 * s + 2)
                wait(pe, s_mx, s)
                for slot in range(2):
                    for k in range(KD):
                        last = pe.transpose(bank[7][:, (slot * KD + k) * P:(slot * KD + k + 1) * P],
                                            cent[:, slot, k * P:(k + 1) * P], ident[:, :])
                last.then_inc(s_cT_ps, 1)

            def product(s):
                pe.wait_ge(s_cT, s + 1)
                for slot in range(2):
                    for k in range(KD):
                        last = pe.matmul(bank[7][:, slot * D:(slot + 1) * D], centT[:, slot, k, :], w1[:, k, :],
                                         start=(k == 0), stop=(k == KD - 1))
                last.then_inc(s_mx_ps, 1)

            flag = pe.value_load(fast[0:1, 0:1], min_val=0, max_val=1)
            with pe.If(flag > 0):
                def scores_of(s, par):
                    pe.wait_ge(s_q, 2 * s + 2)
                    for c in range(HC + 1):
                        b = 1 + (par * (HC + 1) + c) % 2
                        wait(pe, s_qk_used, (HC + 1) * s + c - 1)
                        for k in range(KD):
                            if c < HC:
                                last = three(bank[b][:, :], q_parts, keysU_parts, (every, k, every),
                                             (every, k, slice(c * CH, (c + 1) * CH)), k == 0, k == KD - 1)
                            else:
                                last = pe.matmul(bank[b][:, 0:P], q_low[:, k, :], keysL_t[:, k, s, :],
                                                 start=(k == 0), stop=(k == KD - 1))
                        last.then_inc(s_qk, 1)

                def turn(s, par, c):
                    b = (par * (HC + 1) + c) % 2
                    if c == 0:
                        pe.wait_ge(s_expU, s + 1)
                    if c == HC:
                        pe.wait_ge(s_own_m, s + 1)
                    wait(pe, s_pT, (HC + 1) * s + c - 1)
                    if c < HC:
                        for j in range(BPC):
                            last = pe.transpose(bank[3 + b][:, j * P:(j + 1) * P],
                                                scores[:, par, (c * BPC + j) * P:(c * BPC + j + 1) * P], ident[:, :])
                    else:
                        last = pe.transpose(bank[3 + b][:, 0:P], own[:, par, :], ident[:, :])
                    last.then_inc(s_pT_ps, 1)

                def weigh(s, par, c):
                    b = (par * (HC + 1) + c) % 2
                    pe.wait_ge(s_pT, (HC + 1) * s + c + 1)
                    if c < HC:
                        if c == 0:
                            wait(pe, s_x1, 2 * s - 2)
                        for j in range(BPC):
                            last = pe.matmul(bank[UPPER_BANK[par]][:, 0:D], probT[:, b, j, :],
                                             values[:, HT + c * BPC + j, :],
                                             start=(c == 0 and j == 0), stop=(c == HC - 1 and j == BPC - 1))
                    else:
                        wait(pe, s_x1, 2 * s)
                        last = pe.matmul(bank[6][:, 0:D], probT[:, b, 0, :], values[:, s, :], start=True, stop=True)
                    last.then_inc(s_pv, 1)

                def step(s, par):
                    if not is_step(s, HT - 1):
                        scores_of(s + 1, 1 - par)
                    turn(s, par, 0)
                    turn(s, par, 1)
                    if after(s, 1):
                        product(s - 2)
                    for c in range(HC + 1):
                        weigh(s, par, c)
                        if c + 2 <= HC:
                            turn(s, par, c + 2)
                    if after(s, 0):
                        turn_cent(s - 1)

                scores_of(0, 0)
                pipeline(pe, HT, step, 2)
                product(HT - 2)
                turn_cent(HT - 1)
                product(HT - 1)
            with pe.Else():
                def pair(s, par):
                    for slot in range(2):
                        n = 2 * s + slot
                        pe.wait_ge(s_q, 2 * n + 2)
                        for c in range(NG):
                            wait(pe, g_qk_used, NG * n + c - 1)
                            for k in range(KD):
                                if c < NG // 2:
                                    last = pe.matmul(bank[1 + c % 2][:, :], q_low[:, k, :],
                                                     keysL[:, k, c * CH:(c + 1) * CH], start=(k == 0),
                                                     stop=(k == KD - 1))
                                else:
                                    cu = c - NG // 2
                                    last = three(bank[1 + c % 2][:, :], q_parts, keysU_parts, (every, k, every),
                                                 (every, k, slice(cu * CH, (cu + 1) * CH)), k == 0, k == KD - 1)
                            last.then_inc(g_qk, 1)
                        pe.wait_ge(g_mask, n + 1)
                        for c in range(NG):
                            wait(pe, s_pT, NG * n + c - 1)
                            for j in range(BPC):
                                last = pe.transpose(bank[3 + c % 2][:, j * P:(j + 1) * P],
                                                    adjL[:, 0, (c * BPC + j) * P:(c * BPC + j + 1) * P], ident[:, :])
                            last.then_inc(s_pT_ps, 1)
                            pe.wait_ge(s_pT, NG * n + c + 1)
                            if c == 0:
                                wait(pe, s_x1, n - 1)
                            for j in range(BPC):
                                last = pe.matmul(bank[5 + slot][:, 0:D], probT[:, c % 2, j, :],
                                                 values[:, c * BPC + j, :],
                                                 start=(c == 0 and j == 0), stop=(c == NG - 1 and j == BPC - 1))
                            last.then_inc(s_pv, 1)
                    turn_cent(s)
                    product(s)

                pipeline(pe, HT, pair)

            pe.wait_ge(s_mx, HT)

            def turn_adj(t, par, g):
                if g == 0:
                    pe.wait_ge(d_adj[par], turns(t, par))
                wait(pe, d_lo, NG * t + g - 3)
                for j in range(BPC):
                    last = pe.transpose(bank[g % 4][:, j * P:(j + 1) * P],
                                        adjL[:, par, (g * BPC + j) * P:(g * BPC + j + 1) * P], ident[:, :])
                last.then_inc(d_t_ps, 1)

            def mean_part(t, par, g):
                if g == 0:
                    wait(pe, d_nom, t - 1)
                if is_step(t, 0):
                    pe.wait_ge(s_lo, BPC * (g + 1))
                pe.wait_ge(d_lo, NG * t + g + 1)
                for j in range(BPC):
                    last = three(bank[4 + par][:, 0:XW], (adjT_hi, adjT_lo), (X_hi, X_lo), (every, g % 4, j, every),
                                 (every, g * BPC + j, every), g == 0 and j == 0, g == NG - 1 and j == BPC - 1)
                last.then_inc(d_mm, 1)

            def mean_tile(t, par):
                for g in range(NG):
                    turn_adj(t, par, g)
                    if g >= 2:
                        mean_part(t, par, g - 2)
                    elif after(t, 0):
                        mean_part(t - 1, 1 - par, NG - 2 + g)

            pe.wait_ge(s_edge, 1)
            pipeline(pe, T, mean_tile, 2)
            mean_part(T - 1, 1, NG - 2)
            mean_part(T - 1, 1, NG - 1)

        @block.scalar
        def _(act):
            for n in range(3):
                act.wait_ge(s_wt_ps, n + 1)
                act.copy(wT_hi[:, n].rearrange("p k d -> p (k d)"), bank[n][:, :]).then_inc(s_wt_hi, 1)
            for g in range(NG):
                act.wait_ge(s_grow_ps, g + 1)
                act.copy(graph_row[:, g * CH:(g + 1) * CH], bank[3 + g % 2][:, :]).then_inc(s_grow, 1)

            def deviation(g):
                act.wait_ge(s_var, g + 1)
                act.activation(rstd[:, :], mv[:, :, 1], ACT.Sqrt, bias=ln_eps[:, 0:1]).then_inc(s_std, 1)

            def relu_h(g, par):
                act.wait_ge(s_hT_ps, g + 1)
                wait(act, s_v_ps, 2 * g - 2)
                for k in range(KD):
                    act.activation(hT_hi[:, par, k, :], bank[k][:, :], ACT.Relu).then_inc(s_hT_hi, 1)

            def keys_queries(g):
                for w in range(2):
                    for h in range(KD):
                        act.wait_ge(s_kq_ps, 4 * g + w * KD + h + 1)
                        src = bank[2 + w * KD + h][:, :]
                        gu = g - NG // 2
                        if w == 0:
                            ins = act.activation(qx_v[:, g, :, h * P:(h + 1) * P],
                                                 src.rearrange("p (j c) -> p j c", j=BPC), ACT.Identity,
                                                 bias=bqk[:, 0, h:h + 1], scale=HALF_SCALE)
                        elif gu < 0:
                            ins = act.activation(keysL[:, h, g * CH:(g + 1) * CH], src, ACT.Identity,
                                                 bias=bqk[:, 1, h:h + 1])
                        else:
                            ins = act.activation(keysU_hi[:, h, gu * CH:(gu + 1) * CH], src, ACT.Identity,
                                                 bias=bqk[:, 1, h:h + 1])
                        ins.then_inc(s_kq, 1)

            def project(g, par):
                if g < NG - 1:
                    deviation(g + 1)
                keys_queries(g)
                if g < NG - 1:
                    relu_h(g + 1, 1 - par)

            act.wait_ge(s_const, 1)
            deviation(0)
            relu_h(0, 0)
            for g in range(NG):
                project(g, g % 2)

            def cent_copy(s):
                act.wait_ge(s_cT_ps, s + 1)
                act.copy(centT[:, :, :, :].rearrange("p s k c -> p (s k c)"), bank[7][:, :]).then_inc(s_cT, 1)

            def cent_squares(s, tiles):
                act.wait_ge(s_cent, 2 * s + 2)
                always(act)
                for slot in range(2):
                    last = act.activation(junk[:, slot], cent[:, slot], ACT.Square, accum_out=sq2[:, slot:slot + 1])
                last.then_inc(s_csq, 1)
                act.drain()
                for slot in range(2):
                    act.copy(cent_sq[:, bass.ds(tiles[slot], 1)], sq2[:, slot:slot + 1])

            def product_out(s, tiles, place_of):
                act.wait_ge(s_mx_ps, s + 1)
                always(act)
                for slot in range(2):
                    act.activation(junk[:, 2 + slot], bank[7][:, slot * D:(slot + 1) * D], ACT.Square,
                                   accum_out=sq2[:, 2 + slot:3 + slot])
                act.copy(place_of[:, :, s, 0:D], bank[7][:, :].rearrange("p (h d) -> p h d", h=2)).then_inc(s_mx, 1)
                act.drain()
                for slot in range(2):
                    act.copy(mx_sq[:, bass.ds(tiles[slot], 1)], sq2[:, 2 + slot:3 + slot])

            act.wait_ge(s_fast, 1)
            flag = act.value_load(fast[0:1, 0:1], min_val=0, max_val=1)
            with act.If(flag > 0):
                def exp_upper(s, par):
                    act.wait_ge(s_maxU, s + 1)
                    act.activation(adjU[:, 0:HALF], adjU[:, 0:HALF], ACT.Exp, scale=2.0 * FAR,
                                   bias=neg_top[:, par, 1:2], accum_out=esum[:, par, 1, 0:1])
                    act.activation(scores[:, par, :], scores[:, par, :], ACT.Exp, scale=2.0,
                                   bias=neg_top[:, par, 1:2], accum_out=esum[:, par, 1, 1:2]).then_inc(s_expU, 1)

                def exp_lower(s, par):
                    act.wait_ge(s_maxL, s + 1)
                    act.activation(own[:, par, :], own[:, par, :], ACT.Exp, scale=2.0,
                                   bias=neg_top[:, par, 0:1], accum_out=esum[:, par, 0, 1:2]).then_inc(s_own, 1)
                    act.activation(adjL[:, par], adjL[:, par], ACT.Exp, scale=2.0 * FAR,
                                   bias=neg_top[:, par, 0:1], accum_out=esum[:, par, 0, 0:1]).then_inc(s_expL, 1)

                def step(s, par):
                    for c in range(HC + 1):
                        if c == 2 and after(s, 1):
                            product_out(s - 2, (s - 2, s - 2 + HT), qx_halves)
                        b = (par * (HC + 1) + c) % 2
                        width = CH if c < HC else P
                        act.wait_ge(s_pT_ps, (HC + 1) * s + c + 1)
                        wait(act, s_pv, (HC + 1) * s + c - 1)
                        act.copy(probT[:, b].rearrange("p j c -> p (j c)")[:, 0:width], bank[3 + b][:, 0:width])\
                           .then_inc(s_pT, 1)
                    if after(s, 0):
                        cent_copy(s - 1)
                    if not is_step(s, HT - 1):
                        exp_upper(s + 1, 1 - par)
                    if after(s, 0):
                        cent_squares(s - 1, (s - 1, s - 1 + HT))
                    if not is_step(s, HT - 1):
                        exp_lower(s + 1, 1 - par)

                exp_upper(0, 0)
                exp_lower(0, 0)
                pipeline(act, HT, step, 2)
                product_out(HT - 2, (HT - 2, T - 2), qx_halves)
                cent_copy(HT - 1)
                cent_squares(HT - 1, (HT - 1, T - 1))
                product_out(HT - 1, (HT - 1, T - 1), qx_halves)
            with act.Else():
                def pair(s, par):
                    for slot in range(2):
                        n = 2 * s + slot
                        act.wait_ge(g_max, n + 1)
                        act.activation(adjL[:, 0, :], adjL[:, 0, :], ACT.Exp, scale=2.0, bias=neg_top[:, par, slot:slot + 1],
                                       accum_out=esum[:, par, slot, 0:1]).then_inc(g_exp, 1)
                        for c in range(NG):
                            act.wait_ge(s_pT_ps, NG * n + c + 1)
                            wait(act, s_pv, NG * n + c - 1)
                            act.copy(probT[:, c % 2].rearrange("p j c -> p (j c)"), bank[3 + c % 2][:, :])\
                               .then_inc(s_pT, 1)
                    cent_copy(s)
                    cent_squares(s, (2 * s, 2 * s + 1))
                    product_out(s, (2 * s, 2 * s + 1), qx_pairs)

                pipeline(act, HT, pair)
            act.drain().then_inc(s_var_in, 1)

            done = [0]

            def function(fn, dst, src):
                done[0] += 1
                act.wait_ge(s_f, done[0])
                act.activation(dst[:, :], src[:, :], fn).then_inc(s_fa, 1)

            for fn, i in POINT_FUNCTIONS:
                function(fn, v[i], v[i])
            act.wait_ge(s_f, done[0] + 1)

            def points_high(g):
                for t in range(g * BPC, (g + 1) * BPC):
                    act.activation(X_hi[:, t, 0:D], qx[:, t, 0:D], ACT.Copy, scale=v[8][:, t:t + 1]).then_inc(s_hi, 1)

            def mean_tile(t, par):
                for g in range(NG):
                    if is_step(t, 0):
                        points_high(g)
                    act.wait_ge(d_t_ps, NG * t + g + 1)
                    wait(act, d_mm, NG * t + g - 3)
                    act.copy(adjT_hi[:, g % 4].rearrange("p j c -> p (j c)"), bank[g % 4][:, :]).then_inc(d_hi, 1)
                    if g == 3 and after(t, 0):
                        mean_out(t - 1, 1 - par)
                    if g == 7 and after(t, 0):
                        mean_squares(t - 1, 1 - par)

            def mean_out(t, par):
                act.wait_ge(d_mm, NG * t + NG)
                act.copy(nom[:, par, :], bank[4 + par][:, 0:XW]).then_inc(d_nom, 1)

            def mean_squares(t, par):
                act.wait_ge(d_r, t + 1)
                act.activation(junk[:, 0], nom[:, par, 0:D], ACT.Square, scale=rec[:, par:par + 1],
                               accum_out=sq2[:, 0:1])
                act.activation(junk[:, 1], res[:, t, :], ACT.Square, accum_out=sq2[:, 1:2])
                act.drain()
                act.copy(tm_sq[:, bass.ds(t, 1)], sq2[:, 0:1])
                act.copy(r_sq[:, bass.ds(t, 1)], sq2[:, 1:2])

            pipeline(act, T, mean_tile, 2)
            mean_out(T - 1, 1)
            mean_squares(T - 1, 1)
            act.drain().then_inc(d_sq, 1)
            done[0] += 1
            for fn, i in FINISH_FUNCTIONS:
                function(fn, v[i], v[i])

        @block.vector
        def _(dve):
            dve.memset(ln_eps[:, :], LN_EPS)
            dve.memset(pushed[:, :], PUSHED_OUT)
            for i in range(HT):
                dve.memset(borders[:, i:i + 1], float((i + 1) * P))
            dve.wait_ge(s_ptr, 16)
            dve.tensor_copy(ptr_f[:, :], ptr_i[:, :])
            dve.wait_ge(s_rows, 1)
            dve.tensor_copy(row_no[:, :], row_no_i[:, :])
            dve.wait_ge(s_ident, 3)
            dve.tensor_copy(ident_b[:, :], ident[:, :])
            dve.drain()
            dve.tensor_tensor(counts[:, :, :], row_no[:, :].unsqueeze(2).to_broadcast([P, T, NPTR]),
                              ptr_f[:, :].unsqueeze(1).to_broadcast([P, T, NPTR]), ALU.is_ge)
            dve.drain()
            dve.tensor_reduce(graph_col[:, :], counts[:, :, :], AX.X, ALU.add)
            dve.tensor_tensor(border_eq[:, :, :], borders[:, :].unsqueeze(2).to_broadcast([P, HT, NPTR]),
                              ptr_f[:, :].unsqueeze(1).to_broadcast([P, HT, NPTR]), ALU.is_equal)
            dve.tensor_scalar(in_upper[:, :], ptr_f[:, :], float(HALF), None, ALU.is_gt)
            dve.tensor_scalar(below_end[:, :], ptr_f[:, :], float(N), None, ALU.is_lt)
            dve.drain()
            dve.tensor_reduce(border_hit[:, :], border_eq[:, :, :], AX.X, ALU.max)
            dve.tensor_tensor(in_upper[:, :], in_upper[:, :], below_end[:, :], ALU.mult)
            dve.drain()
            dve.tensor_reduce(checks[:, 0:1], border_hit[:, :], AX.X, ALU.add)
            dve.tensor_reduce(checks[:, 1:2], in_upper[:, :], AX.X, ALU.add)
            dve.drain()
            dve.tensor_tensor(checks[:, 2:3], checks[:, 0:1], checks[:, 1:2], ALU.subtract)
            dve.drain()
            dve.tensor_scalar(fast[:, :], checks[:, 2:3], float(HT), None, ALU.is_ge).then_inc(s_fast, 1)
            for g in range(NG):
                wait(dve, s_grow_ps, g - 1)
                for j in range(BPC):
                    t = g * BPC + j
                    last = dve.tensor_scalar(diag[:, g % 2, j * P:(j + 1) * P], ident_b[:, :],
                                             graph_col[:, t:t + 1], None, ALU.mult)
                last.then_inc(s_diag, 1)
            dve.wait_ge(s_w, 16 * 8)
            dve.tensor_scalar(bqk[:, 0], bqk[:, 0], HALF_SCALE, None, ALU.mult).then_inc(s_const, 1)

            def normalise(g, par):
                if isinstance(g, int):
                    dve.wait_ge(s_xin[par], 16 * (g // 2 + 1))
                else:
                    dve.wait_ge(s_xin[par], g * 8 - 8 * par + 16)
                for j in range(BPC):
                    dve.bn_stats(bnst[:, j, :], xin[:, par, j, :])
                dve.drain()
                for j in range(BPC):
                    last = dve.bn_aggr(mv[:, j, :], bnst[:, j, :])
                last.then_inc(s_var, 1)
                dve.wait_ge(s_std, g + 1)
                dve.reciprocal(rstd[:, :], rstd[:, :])
                dve.drain()
                for j in range(BPC):
                    last = dve.tensor_scalar(xin[:, par, j, :], xin[:, par, j, :], mv[:, j, 0:1], rstd[:, j:j + 1],
                                             ALU.subtract, ALU.mult)
                last.then_inc(s_norm, 1)

            def low_h(g, par):
                for k in range(KD):
                    dve.wait_ge(s_hT_hi, KD * g + k + 1)
                    dve.scalar_tensor_tensor(out=hT_lo[:, par, k, :], in0=bank[k][:, :], scalar=0.0,
                                             in1=hT_hi[:, par, k, :].bitcast(F32), op0=ALU.max,
                                             op1=ALU.subtract).then_inc(s_hT, 1)

            def project(g, par):
                if g < NG - 1:
                    normalise(g + 1, 1 - par)
                gu = g - NG // 2
                if gu >= 0:
                    for h in range(KD):
                        dve.wait_ge(s_kq, 4 * g + KD + h + 1)
                        dve.scalar_tensor_tensor(out=keysU_lo[:, h, gu * CH:(gu + 1) * CH], in0=bank[2 + KD + h][:, :],
                                                 scalar=bqk[:, 1, h:h + 1],
                                                 in1=keysU_hi[:, h, gu * CH:(gu + 1) * CH].bitcast(F32),
                                                 op0=ALU.add, op1=ALU.subtract).then_inc(s_key_lo, 1)
                if g < NG - 1:
                    low_h(g + 1, 1 - par)
                for b in range(2):
                    dve.wait_ge(s_v_ps, 2 * g + b + 1)
                    dve.tensor_tensor(val_v[:, g, 2 * b:2 * b + 2, :], bank[6 + b][:, :].rearrange("p (j d) -> p j d", j=2),
                                      bv_row[:, :, :], ALU.add).then_inc(s_v, 1)

            for n in range(3):
                dve.wait_ge(s_wt_hi, n + 1)
                dve.tensor_tensor(wT_lo[:, n].rearrange("p k d -> p (k d)"), bank[n][:, :],
                                  wT_hi[:, n].rearrange("p k d -> p (k d)").bitcast(F32), ALU.subtract)\
                   .then_inc(s_wt, 1)
            normalise(0, 0)
            low_h(0, 0)
            for g in range(NG):
                project(g, g % 2)

            def tile_out(groups, s, par, slot, t, b, one_sum):
                dve.wait_ge(s_pv, groups)
                if one_sum:
                    dve.reciprocal(tot[:, slot:slot + 1], esum[:, par, slot, 0:1])
                else:
                    dve.tensor_tensor(tot[:, slot:slot + 1], esum[:, par, slot, 0:1], esum[:, par, slot, 1:2], ALU.add)
                    dve.drain()
                    dve.reciprocal(tot[:, slot:slot + 1], tot[:, slot:slot + 1])
                dve.drain()
                dve.wait_ge(s_xt[par], turns(s, par))
                wait(dve, s_x1_out, 16 * s)
                dve.scalar_tensor_tensor(out=x1[:, slot], in0=bank[b][:, 0:D], scalar=tot[:, slot:slot + 1],
                                         in1=xt[:, par, slot], op0=ALU.mult, op1=ALU.add).then_inc(s_x1, 1)
                dve.drain()
                dve.bn_stats(bn1[:, :], x1[:, slot])
                dve.drain()
                dve.bn_aggr(mv1[:, :], bn1[:, :])
                dve.drain()
                dve.tensor_copy(var_all[:, bass.ds(t, 1)], mv1[:, 1:2])
                wait(dve, s_cT_ps, s)
                wait(dve, s_csq, s)
                dve.tensor_scalar(cent[:, slot], x1[:, slot], mv1[:, 0:1], 0.0, ALU.subtract, ALU.max).then_inc(s_cent, 1)

            dve.wait_ge(s_grow, NG)
            flag = dve.value_load(fast[0:1, 0:1], min_val=0, max_val=1)
            with dve.If(flag > 0):
                def scores_upper(s, par):
                    dve.wait_ge(s_window, 16 * s + 16)
                    wait(dve, s_pT_ps, (HC + 1) * (s - 2) + HC)
                    for c in range(HC):
                        dve.wait_ge(s_qk, (HC + 1) * s + c + 1)
                        dve.sem_inc(s_seen, 1)
                        dve.tensor_tensor_reduce(out=scores[:, par, c * CH:(c + 1) * CH],
                                                 in0=adjU[:, HALF + c * CH:HALF + (c + 1) * CH],
                                                 in1=bank[1 + (par * (HC + 1) + c) % 2][:, :], scale=1.0,
                                                 scalar=-3.0e38, op0=ALU.add, op1=ALU.max,
                                                 accum_out=mx[:, c:c + 1]).then_inc(s_qk_used, 1)

                def scores_lower(s, par):
                    wait(dve, s_own_m, s - 1)
                    dve.tensor_scalar(same[:, par, :], graph_t[:, s, :], graph_col[:, bass.ds(s, 1)], None, ALU.is_equal)
                    dve.drain()
                    dve.tensor_scalar(factor[:, :], same[:, par, :], 1.0 - FAR, FAR, ALU.mult, ALU.add)
                    dve.wait_ge(s_qk, (HC + 1) * s + HC + 1)
                    dve.tensor_tensor(near_part[:, :], same[:, par, :], bank[1 + (par * (HC + 1) + HC) % 2][:, 0:P],
                                      ALU.mult).then_inc(s_qk_used, 1)

                def maximum(par, slot, done):
                    dve.drain()
                    dve.scalar_tensor_tensor(out=top[:, :], in0=least[:, :], scalar=FAR, in1=top[:, :],
                                             op0=ALU.mult, op1=ALU.max)
                    dve.drain()
                    dve.tensor_scalar(neg_top[:, par, slot:slot + 1], top[:, :], -2.0, None, ALU.mult).then_inc(done, 1)

                def maximum_upper(s, par):
                    dve.wait_ge(s_beside, 16 * s + 16)
                    dve.tensor_reduce(least[:, :], adjU[:, 0:HALF], AX.X, ALU.min)
                    dve.tensor_reduce(top[:, :], mx[:, 0:HC], AX.X, ALU.max)
                    maximum(par, 1, s_maxU)

                def maximum_lower(s, par):
                    dve.wait_ge(s_adjL[par], turns(s, par))
                    dve.tensor_tensor(far_part[:, :], adjL_t[:, par, s, :], factor[:, :], ALU.mult)
                    dve.drain()
                    dve.tensor_copy(adjL_t[:, par, s, :], pushed[:, :])
                    dve.drain()
                    wait(dve, s_pT_ps, (HC + 1) * (s - 1))
                    dve.sem_inc(s_seen, 1)
                    dve.tensor_tensor_reduce(out=own[:, par, :], in0=far_part[:, :], in1=near_part[:, :], scale=1.0,
                                             scalar=-3.0e38, op0=ALU.add, op1=ALU.max, accum_out=top[:, :])
                    dve.tensor_reduce(least[:, :], adjL[:, par], AX.X, ALU.min)
                    maximum(par, 0, s_maxL)

                def tiles_out(s, par):
                    tile_out((HC + 1) * s + HC, s, par, 1, s + HT, UPPER_BANK[par], False)
                    tile_out((HC + 1) * s + HC + 1, s, par, 0, s, 6, False)

                def step(s, par):
                    if not is_step(s, HT - 1):
                        scores_upper(s + 1, 1 - par)
                        scores_lower(s + 1, 1 - par)
                    if after(s, 0):
                        tiles_out(s - 1, 1 - par)
                    if not is_step(s, HT - 1):
                        maximum_upper(s + 1, 1 - par)
                        maximum_lower(s + 1, 1 - par)

                scores_upper(0, 0)
                scores_lower(0, 0)
                maximum_upper(0, 0)
                maximum_lower(0, 0)
                pipeline(dve, HT, step, 2)
                tiles_out(HT - 1, 1)
            with dve.Else():
                def pair(s, par):
                    for slot in range(2):
                        n = 2 * s + slot
                        dve.wait_ge(g_adj, 16 * n + 16)
                        for c in range(NG):
                            cols = slice(c * CH, (c + 1) * CH)
                            dve.tensor_scalar(mask_c[:, :], graph_row[:, cols], graph_col[:, bass.ds(n, 1)], None, ALU.is_equal)
                            dve.drain()
                            dve.tensor_scalar(factor_c[:, :], mask_c[:, :], 1.0 - FAR, FAR, ALU.mult, ALU.add)
                            dve.wait_ge(g_qk, NG * n + c + 1)
                            dve.tensor_tensor(near_c[:, :], mask_c[:, :], bank[1 + c % 2][:, :], ALU.mult).then_inc(g_qk_used, 1)
                            dve.drain()
                            dve.tensor_tensor(adjL[:, 0, cols], adjL[:, 0, cols], factor_c[:, :], ALU.mult)
                            dve.drain()
                            dve.tensor_tensor_reduce(out=adjL[:, 0, cols], in0=adjL[:, 0, cols], in1=near_c[:, :], scale=1.0,
                                                     scalar=-3.0e38, op0=ALU.add, op1=ALU.max, accum_out=mx[:, c:c + 1])
                            dve.drain()
                        dve.tensor_reduce(top[:, :], mx[:, 0:NG], AX.X, ALU.max)
                        dve.drain()
                        dve.tensor_scalar(neg_top[:, par, slot:slot + 1], top[:, :], -2.0, None, ALU.mult).then_inc(g_max, 1)
                        dve.wait_ge(g_exp, n + 1)
                        for c in range(NG):
                            cols = slice(c * CH, (c + 1) * CH)
                            dve.tensor_scalar(mask_c[:, :], graph_row[:, cols], graph_col[:, bass.ds(n, 1)], None, ALU.is_equal)
                            dve.drain()
                            dve.tensor_tensor(adjL[:, 0, cols], adjL[:, 0, cols], mask_c[:, :], ALU.mult)
                            dve.drain()
                        dve.drain().then_inc(g_mask, 1)
                        tile_out(NG * n + NG, s, par, slot, n, 5 + slot, True)

                pipeline(dve, HT, pair)

            asked = [0]
            taken = [0]

            def function(last):
                last.then_inc(s_f, 1)
                asked[0] += 1
                dve.wait_ge(s_fa, asked[0])

            def ts(o, a, s1, s2, op0, op1=ALU.bypass):
                last = dve.tensor_scalar(o, a, s1, s2, op0, op1) if s2 is not None else dve.tensor_scalar(o, a, s1, None, op0)
                return last

            def tt(o, a, b, op):
                return dve.tensor_tensor(o, a, b, op)

            def artanh(o, a, t1, t2, t3, fn):
                ts(t1, a, -1.0, 1.0, ALU.mult, ALU.add)
                ts(t2, a, 1.0, None, ALU.add)
                dve.drain()
                dve.reciprocal(t1, t1)
                dve.drain()
                fn(tt(t1, t1, t2, ALU.mult))
                tt(t2, a, a, ALU.mult)
                dve.drain()
                ts(t3, t2, 1.0 / 13, None, ALU.mult)
                for c in (11, 9, 7, 5, 3):
                    dve.drain()
                    dve.scalar_tensor_tensor(out=t3, in0=t3, scalar=1.0 / c, in1=t2, op0=ALU.add, op1=ALU.mult)
                dve.drain()
                dve.scalar_tensor_tensor(out=t3, in0=t3, scalar=1.0, in1=a, op0=ALU.add, op1=ALU.mult)
                ts(t1, t1, 0.5, None, ALU.mult)
                ts(t2, a, TINY_ARG, None, ALU.is_lt)
                dve.drain()
                tt(t3, t3, t1, ALU.subtract)
                dve.drain()
                tt(t3, t3, t2, ALU.mult)
                dve.drain()
                tt(o, t1, t3, ALU.add)
                dve.drain()

            V = [a[:, :] for a in v]
            dve.drain()
            dve.wait_ge(s_var_in, 1)
            function(ts(V[0], var_all[:, :], LN_EPS, None, ALU.add))
            dve.reciprocal(V[0], V[0])
            dve.drain()
            tt(V[3], V[0], V[0], ALU.mult)
            dve.drain()
            tt(V[1], V[3], cent_sq[:, :], ALU.mult)
            tt(V[4], V[3], mx_sq[:, :], ALU.mult)
            dve.drain()
            function(ts(V[1], V[1], FLOOR, None, ALU.max))
            function(ts(V[2], V[4], FLOOR, None, ALU.max))
            ts(V[3], V[1], CLIP, None, ALU.min)
            dve.drain()
            artanh(V[3], V[3], V[5], V[6], V[7], function)
            dve.reciprocal(V[1], V[1])
            tt(V[3], V[3], V[2], ALU.mult)
            dve.drain()
            function(tt(V[3], V[3], V[1], ALU.mult))
            dve.reciprocal(V[2], V[2])
            ts(V[4], V[4], FLOOR, None, ALU.is_gt)
            dve.drain()
            tt(V[3], V[3], V[2], ALU.mult)
            tt(V[4], V[4], V[0], ALU.mult)
            dve.drain()
            tt(V[3], V[3], V[4], ALU.mult)
            dve.drain()
            tt(V[4], V[3], V[3], ALU.mult)
            dve.drain()
            tt(V[4], V[4], mx_sq[:, :], ALU.mult)
            dve.drain()
            ts(V[4], V[4], -1.0, 1.0, ALU.mult, ALU.add)
            dve.drain()
            dve.reciprocal(V[4], V[4])
            dve.drain()
            ts(V[4], V[4], 2.0, 1e-15, ALU.mult, ALU.max)
            dve.drain()
            tt(V[8], V[3], V[4], ALU.mult).then_inc(s_f, 1)
            ts(V[5], V[4], -1.0, None, ALU.add)
            dve.memset(V[6], 1.0)
            dve.memset(V[7], 0.0)
            dve.drain()
            dve.tensor_copy(X_hi[:, :, D], V[5])
            dve.tensor_copy(X_hi[:, :, D + 1], V[6])
            dve.tensor_copy(X_lo[:, :, D + 1], V[7])
            dve.drain()
            tt(X_lo[:, :, D], V[5], X_hi[:, :, D].bitcast(F32), ALU.subtract).then_inc(s_edge, 1)

            def points_low(g):
                for t in range(g * BPC, (g + 1) * BPC):
                    dve.wait_ge(s_hi, t + 1)
                    dve.scalar_tensor_tensor(out=X_lo[:, t, 0:D], in0=qx[:, t, 0:D], scalar=v[8][:, t:t + 1],
                                             in1=X_hi[:, t, 0:D].bitcast(F32), op0=ALU.mult,
                                             op1=ALU.subtract).then_inc(s_lo, 1)

            def mean_tile(t, par):
                for g in range(NG):
                    if is_step(t, 0):
                        points_low(g)
                    dve.wait_ge(d_hi, NG * t + g + 1)
                    dve.tensor_tensor(adjT_lo[:, g % 4].rearrange("p j c -> p (j c)"), bank[g % 4][:, :],
                                      adjT_hi[:, g % 4].rearrange("p j c -> p (j c)").bitcast(F32),
                                      ALU.subtract).then_inc(d_lo, 1)
                    if g == 5 and after(t, 0):
                        mean_relu(t - 1, 1 - par)

            def mean_relu(t, par):
                dve.wait_ge(d_nom, t + 1)
                ts(sgn[:, :], nom[:, par, D:D + 2], 0.0, 2.0, ALU.is_ge, ALU.mult)
                dve.drain()
                ts(sgn[:, :], sgn[:, :], -1.0, None, ALU.add)
                dve.drain()
                tt(size[:, :], nom[:, par, D:D + 2], sgn[:, :], ALU.mult)
                dve.drain()
                ts(rec[:, par:par + 1], size[:, 0:1], EPS, None, ALU.max)
                dve.tensor_copy(alpha[:, bass.ds(t, 1)], size[:, 1:2])
                dve.drain()
                dve.reciprocal(rec[:, par:par + 1], rec[:, par:par + 1])
                dve.drain()
                dve.scalar_tensor_tensor(out=turn[:, 0:1], in0=sgn[:, 0:1], scalar=sgn[:, 1:2],
                                         in1=rec[:, par:par + 1], op0=ALU.mult, op1=ALU.mult)
                dve.drain()
                ts(res[:, t, :], nom[:, par, 0:D], turn[:, 0:1], 0.0, ALU.mult, ALU.max).then_inc(d_r, 1)

            pipeline(dve, T, mean_tile, 2)
            mean_relu(T - 1, 1)

            dve.drain()
            dve.wait_ge(d_sq, 1)
            ts(V[0], tm_sq[:, :], -1.0, 1.0, ALU.mult, ALU.add)
            dve.drain()
            function(ts(V[0], V[0], EPS, None, ALU.max))
            ts(V[0], V[0], 1.0, None, ALU.add)
            dve.drain()
            dve.reciprocal(V[0], V[0])
            dve.drain()
            tt(V[1], V[0], V[0], ALU.mult)
            dve.drain()
            tt(V[1], V[1], tm_sq[:, :], ALU.mult)
            dve.drain()
            function(ts(V[1], V[1], FLOOR, None, ALU.max))
            ts(V[2], V[1], CLIP, None, ALU.min)
            dve.drain()
            artanh(V[2], V[2], V[5], V[6], V[7], function)
            function(tt(V[2], V[2], alpha[:, :], ALU.mult))
            dve.reciprocal(V[1], V[1])
            tt(V[0], V[0], V[2], ALU.mult)
            dve.drain()
            tt(V[0], V[0], V[1], ALU.mult)
            dve.drain()
            tt(V[1], V[0], V[0], ALU.mult)
            dve.drain()
            tt(V[1], V[1], tm_sq[:, :], ALU.mult)
            dve.drain()
            function(ts(V[1], V[1], FLOOR, None, ALU.max))
            ts(V[2], V[1], CLIP, None, ALU.min)
            dve.drain()
            artanh(V[2], V[2], V[5], V[6], V[7], function)
            dve.reciprocal(V[1], V[1])
            tt(V[0], V[0], V[2], ALU.mult)
            dve.drain()
            tt(V[0], V[0], V[1], ALU.mult)
            dve.drain()
            tt(V[1], V[0], V[0], ALU.mult)
            dve.drain()
            tt(V[1], V[1], r_sq[:, :], ALU.mult)
            dve.drain()
            function(ts(V[1], V[1], FLOOR, None, ALU.max))
            dve.reciprocal(V[3], V[1])
            dve.drain()
            function(tt(V[1], V[1], V[1], ALU.max))
            tt(V[0], V[0], V[3], ALU.mult)
            dve.drain()
            tt(V[0], V[0], V[1], ALU.mult)
            dve.drain()
            dve.wait_ge(s_x1_all, 16 * 4)
            for g in range(NG):
                for j in range(BPC):
                    t = g * BPC + j
                    last = dve.scalar_tensor_tensor(out=res[:, t, :], in0=res[:, t, :], scalar=v[0][:, t:t + 1],
                                                    in1=x1_all[:, t, :], op0=ALU.mult, op1=ALU.add)
                last.then_inc(s_out, 1)


_INS = ["x", "adj", "L0_gnn_ptr", "L0_gnn_Wq", "L0_gnn_bq", "L0_gnn_Wk", "L0_gnn_bk", "L0_gnn_Wv", "L0_gnn_bv",
        "L1_gnn_W"]


def kernel(**inputs):
    import numpy as _np
    import concourse.bacc as _bacc
    from concourse import mybir as _mybir
    from concourse.bass_utils import run_bass_kernel_spmd as _run

    nc = _bacc.Bacc("TRN2", target_bir_lowering=False, num_devices=1, dynamic_dma_scratch_size=1024)
    arrays, args = {}, []
    for name in _INS:
        a = _np.ascontiguousarray(inputs[name])
        arrays[f"in_{name}"] = a
        args.append(nc.dram_tensor(f"in_{name}", a.shape, _mybir.dt.from_np(a.dtype), kind="ExternalInput").ap())
    shape = inputs["x"].shape
    args.append(nc.dram_tensor("out_x", shape, _mybir.dt.float32, kind="ExternalOutput").ap())
    graph_layers_kernel(nc, *args)
    r = _run(nc, [arrays], core_ids=[0])
    return r.results[0]["out_x"]
```

```python
import concourse.bass as bass
from concourse import mybir
from contextlib import ExitStack

F32 = mybir.dt.float32
BF16 = mybir.dt.bfloat16
F32R = mybir.dt.float32r
I32 = mybir.dt.int32
ALU = mybir.AluOpType
ACT = mybir.ActivationFunctionType
AX = mybir.AxisListType

P = 128
LN_EPS = 1e-5
FAR = -1.0e6
EPS = 1e-10
CLIP = 1.0 - 1e-7
TINY_ARG = 0.25
PUSHED_OUT = 1.0e30


UPPER_BANK = (5, 0)

POINT_FUNCTIONS = [(ACT.Sqrt, "squares", "roots"), (ACT.Ln, 5, 5), (ACT.Tanh, 3, 3)]
FINISH_FUNCTIONS = [(ACT.Sqrt, "squares", "roots"), (ACT.Ln, 5, 5), (ACT.Tanh, 2, 2), (ACT.Ln, 5, 5),
                    (ACT.Tanh, 1, 3)]
FINISH_GROUPS = (1, 3, 7, 9, 13)
LATE = 5


def graph_layers_kernel(nc, x, adj, ptr, Wq, bq, Wk, bk, Wv, bv, W, out):
    N, D = x.shape
    T = N // P
    HT = T // 2
    KD = D // P
    CH = 512
    BPC = CH // P
    NG = N // CH
    HALF = N // 2
    HC = HALF // CH
    NPTR = ptr.shape[0]
    EARLY = HT - BPC
    POINT_GROUPS = [g for g in range(NG) if g % (NG // 2) != NG // 2 - 1] + [NG // 2 - 1, NG - 1]
    XW = D + 2
    HALF_SCALE = 0.5 / float(D) ** 0.5

    x_g = x.rearrange("(g j p) d -> g p j d", p=P, j=BPC)
    x_halves = x.rearrange("(h s p) d -> s p h d", p=P, h=2)
    x_pairs = x.rearrange("(s h p) d -> s p h d", p=P, h=2)
    adj_t = adj.rearrange("(t p) n -> t p n", p=P)
    out_g = out.rearrange("(g j p) d -> g p j d", p=P, j=BPC)

    ctx = ExitStack()
    with ctx:
        def sb(name, shape, dt=F32):
            return ctx.enter_context(nc.sbuf_tensor(name, shape, dt))

        def sem(name):
            return ctx.enter_context(nc.semaphore(name))

        x1_dram = nc.dram_tensor("x1_scratch", [N, D], F32, kind="Internal").ap()
        x1_halves = x1_dram.rearrange("(h s p) d -> s p h d", p=P, h=2)
        x1_pairs = x1_dram.rearrange("(s h p) d -> s p h d", p=P, h=2)

        w1 = sb("w1", [P, KD, D])
        bqk = sb("bqk", [P, 2, KD])
        bv_row = sb("bv_row", [P, 2, D])
        junk = sb("junk", [P, 4, D], BF16)
        ident = sb("ident", [P, P])
        ident_b = sb("ident_b", [P, P], BF16)
        ones_b = sb("ones_b", [P, P], BF16)
        diag = sb("diag", [P, 2, CH], BF16)
        graph_col = sb("graph_col", [P, T])
        row_no = sb("row_no", [P, T])
        row_no_i = sb("row_no_i", [P, T], I32)
        ptr_i = sb("ptr_i", [P, NPTR], I32)
        ptr_f = sb("ptr_f", [P, NPTR])
        in_upper = sb("in_upper", [P, NPTR])
        below_end = sb("below_end", [P, NPTR])
        borders = sb("borders", [P, HT])
        border_hit = sb("border_hit", [P, HT])
        checks = sb("checks", [P, 4])
        fast = sb("fast", [P, 1], I32)
        ln_eps = sb("ln_eps", [P, 1])
        bnst = sb("bnst", [P, BPC, 6])
        mv = sb("mv", [P, BPC, 2])
        rstd = sb("rstd", [P, BPC])
        mx = sb("mx", [P, 8])
        top = sb("top", [P, 1])
        least = sb("least", [P, 1])
        neg_top = sb("neg_top", [P, 2, 2])
        esum = sb("esum", [P, 2, 2, 2])
        tot = sb("tot", [P, 2])
        bn1 = sb("bn1", [P, 2, 6])
        mv1 = sb("mv1", [P, 2, 2])
        point_sq = sb("point_sq", [P, 3, T])
        sq2 = sb("sq2", [P, 4])
        mean_sq = sb("mean_sq", [P, 3, T])
        roots = sb("roots", [P, 3, T])
        alpha = sb("alpha", [P, T])
        v = [sb(f"v{i}", [P, T]) for i in range(9)]
        rec = sb("rec", [P, 2])
        sgn = sb("sgn", [P, 2])
        size = sb("size", [P, 2])
        turn = sb("turn", [P, 2])

        region, at = {}, -(-nc.sbuf_base // 32) * 32
        for name, size_b in (("keys", 3 * KD * HALF * 4), ("values", T * D * 4), ("qx", T * XW * 4),
                             ("graph", N * 2), ("adjL", 2 * N * 4), ("scores", 2 * HALF * 4),
                             ("adjU", N * 4), ("small", 46 * P * 4)):
            region[name] = at
            at += -(-size_b // 32) * 32

        def place(name, shape, where, offset=0, dt=F32):
            return nc.alloc_sbuf_tensor_at(name, shape, dt, offset=region[where] + offset)

        values = place("values", [P, T, D], "values")
        qx = place("qx", [P, T, XW], "qx")
        graph_row = place("graph_row", [P, N], "graph", dt=BF16)
        xin = place("xin", [P, 2, BPC, D], "adjL", N * 4)
        w_raw = place("w_raw", [P, 3, KD, D], "scores")
        counts = place("counts", [P, T, NPTR], "adjU")
        border_eq = place("border_eq", [P, HT, NPTR], "adjL")
        small = iter(range(0, 46 * P * 4, P * 4))

        def place_small(name, shape, dt=F32):
            words = 1
            for n in shape[1:]:
                words *= n
            first = next(small)
            for _ in range(words // P - 1):
                next(small)
            return place(name, shape, "small", first, dt)

        probT = place_small("probT", [P, 2, BPC, P])
        xt = place_small("xt", [P, 2, 2, D])
        x1 = place_small("x1", [P, 2, D])
        cent = place_small("cent", [P, 2, D])
        centT = place_small("centT", [P, 2, KD, P])
        own = place_small("own", [P, 2, P])
        same = place_small("same", [P, 2, P])
        factor = place_small("factor", [P, P])
        far_part = place_small("far_part", [P, P])
        near_part = place_small("near_part", [P, P])
        pushed = place_small("pushed", [P, P])
        q_low = place_small("q_low", [P, KD, P])
        stage_at = next(small)
        q_hi = place("q_hi", [P, KD, P], "small", stage_at, F32R)
        q_lo = place("q_lo", [P, KD, P], "small", stage_at + KD * P * 4, F32R)
        keysU_hi = place("keysU_hi", [P, KD, HALF], "keys", 0, F32R)
        keysU_lo = place("keysU_lo", [P, KD, HALF], "keys", KD * HALF * 4, F32R)
        keysL = place("keysL", [P, KD, HALF], "keys", 2 * KD * HALF * 4)
        hT_hi = place("hT_hi", [P, 2, KD, CH], "scores", 0, F32R)
        hT_lo = place("hT_lo", [P, 2, KD, CH], "scores", 2 * KD * CH * 4, F32R)
        wT_hi = place("wT_hi", [P, 3, KD, D], "adjL", N * 4 + 2 * BPC * D * 4, F32R)
        wT_lo = place("wT_lo", [P, 3, KD, D], "small", 0, F32R)
        adjL = place("adjL", [P, 2, N], "adjL")
        adjU = place("adjU", [P, N], "adjU")
        scores = place("scores", [P, 2, HALF], "scores")
        mask_c = place("mask_c", [P, CH], "scores")
        factor_c = place("factor_c", [P, CH], "scores", CH * 4)
        near_c = place("near_c", [P, CH], "scores", 2 * CH * 4)
        X_hi = place("X_hi", [P, T, XW], "keys", 0, F32R)
        X_lo = place("X_lo", [P, T, XW], "keys", T * XW * 4, F32R)
        adjT_hi = place("adjT_hi", [P, 4, BPC, P], "keys", 2 * T * XW * 4, F32R)
        adjT_lo = place("adjT_lo", [P, 4, BPC, P], "scores", 0, F32R)
        nom = place("nom", [P, 2, XW], "scores", 4 * BPC * P * 4)
        res = place("res", [P, T, D], "adjU")
        x1_all = place("x1_all", [P, T, D], "qx")

        qx_v = qx[:, :, :].rearrange("p (g j) c -> p g j c", j=BPC)
        halves = lambda a: a.rearrange("p (h s) -> p h s", h=2)
        EARLY_COLS = (slice(None), slice(None), slice(0, EARLY))
        LAST_COLS = (slice(None), slice(None), slice(EARLY, HT))
        var_halves, var_pairs = (point_sq[:, 0].rearrange(a, h=2) for a in ("p (h s) -> p h s", "p (s h) -> p h s"))
        csq_halves, csq_pairs = (point_sq[:, 1].rearrange(a, h=2) for a in ("p (h s) -> p h s", "p (s h) -> p h s"))
        msq_halves, msq_pairs = (point_sq[:, 2].rearrange(a, h=2) for a in ("p (h s) -> p h s", "p (s h) -> p h s"))
        qx_halves = qx[:, :, :].rearrange("p (h s) c -> p h s c", h=2)
        qx_pairs = qx[:, :, :].rearrange("p (s h) c -> p h s c", h=2)
        val_v = values[:, :, :].rearrange("p (g j) d -> p g j d", j=BPC)
        keysL_t = keysL[:, :, :].rearrange("p k (t c) -> p k t c", c=P)
        graph_t = graph_row[:, :].rearrange("p (t c) -> p t c", c=P)
        adjL_t = adjL[:, :, :].rearrange("p a (t c) -> p a t c", c=P)

        bank = [ctx.enter_context(nc.psum_tensor(f"bank{i}", [P, CH], F32)) for i in range(8)]

        s_ptr = sem("ptr_in")
        s_w = sem("weights_in")
        s_small = sem("biases_and_last_weights_in")
        s_xin = [sem("x_group_in0"), sem("x_group_in1")]
        s_ident = sem("ident_ready")
        s_rows = sem("row_numbers_ready")
        s_const = sem("vector_constants_ready")
        s_wt_ps = sem("weights_turned")
        s_wt_hi = sem("turned_weights_high_ready")
        s_wt = sem("turned_weights_ready")
        s_diag = sem("diag_ready")
        s_grow_ps = sem("graph_row_in_psum")
        s_grow = sem("graph_row_copied")
        s_fast = sem("path_chosen")
        s_var = sem("variance_ready")
        s_std = sem("deviation_ready")
        s_norm = sem("normalised")
        s_hT_ps = sem("h_turned")
        s_hT_hi = sem("hT_high_ready")
        s_hT = sem("hT_ready")
        s_kq_ps = sem("keys_queries_in_psum")
        s_kq = sem("keys_queries_copied")
        s_key_lo = sem("upper_keys_low_ready")
        s_v_ps = sem("values_in_psum")
        s_v = sem("values_copied")
        s_window = sem("adj_upper_window_in")
        s_beside = sem("adj_upper_rest_in")
        s_adjL = [sem("adj_lower_in0"), sem("adj_lower_in1")]
        s_xt = [sem("x_pair_in0"), sem("x_pair_in1")]
        s_x1_out = sem("x1_stored")
        s_q = sem("queries_staged")
        s_qk = sem("scores_in_psum")
        s_qk_used = sem("scores_read")
        s_seen = sem("waits_carried_for_reduces")
        s_sync_seen = sem("waits_carried_for_addresses")
        s_maxU = sem("upper_maximum_ready")
        s_maxL = sem("lower_maximum_ready")
        s_expB = sem("upper_rest_exp_done")
        s_expU = sem("upper_exp_done")
        s_own = sem("own_exp_done")
        s_own_m = sem("own_exp_masked")
        s_expL = sem("lower_exp_done")
        s_pT_ps = sem("exp_turned")
        s_pT = sem("turned_exp_copied")
        s_pv = sem("group_of_values_summed")
        s_x1 = sem("x1_ready")
        s_cent = sem("centred_ready")
        s_csq = sem("centred_squared")
        s_cT_ps = sem("centred_turned")
        s_cT = sem("centred_copied")
        s_mx_ps = sem("product_in_psum")
        s_mx = sem("product_copied")
        g_adj = sem("general_adj_in")
        g_qk = sem("general_scores_in_psum")
        g_qk_used = sem("general_scores_read")
        g_max = sem("general_maximum_ready")
        g_exp = sem("general_exp_done")
        g_mask = sem("general_exp_masked")
        s_f = sem("factor_step")
        s_fa = sem("factor_function")
        s_msq = sem("squares_of_pair_kept")
        s_edge = sem("last_columns_ready")
        s_hi = sem("points_high_ready")
        s_lo = sem("points_low_ready")
        d_adj = [sem("mean_adj_in0"), sem("mean_adj_in1")]
        d_t_ps = sem("adj_turned")
        d_hi = sem("turned_adj_high_ready")
        d_lo = sem("turned_adj_low_ready")
        d_mm = sem("group_of_mean_summed")
        d_nom = sem("mean_copied")
        d_r = sem("mean_relu_ready")
        d_sq = sem("mean_squares_ready")
        s_x1_all = sem("x1_back")
        s_out = sem("out_group_ready")
        s_stored = sem("out_stored")

        def wait(eng, s, value):
            if not isinstance(value, int) or value > 0:
                eng.wait_ge(s, value)

        def always(eng):
            eng.wait_ge(s_ident, 3)

        def pipeline(eng, n, step, peel=1, unroll=2):
            for s in range(peel):
                step(s, s % 2)
            with eng.Fori(0, (n - 2 * peel) // unroll) as i:
                for j in range(unroll):
                    step(unroll * i + peel + j, (peel + j) % 2)
            for s in range(n - peel, n):
                step(s, s % 2)

        def is_step(s, value):
            return isinstance(s, int) and s == value

        def after(s, value):
            return not isinstance(s, int) or s > value

        def group_order(t):
            return POINT_GROUPS if is_step(t, 0) else list(range(NG))

        def turns(s, par):
            return 16 * ((s - par) // 2 + 1) if isinstance(s, int) else s * 8 - 8 * par + 16

        block = ctx.enter_context(nc.Block())

        @block.sync
        def _(sp):
            sp.dma_start(ptr_i[:, :], ptr.rearrange("(a k) -> a k", a=1).partition_broadcast(P)).then_inc(s_ptr, 16)
            sp.dma_start(xin[:, 0], x_g[0]).then_inc(s_xin[0], 16)
            for n, w in enumerate((Wq, Wk, Wv)):
                sp.dma_start(w_raw[:, n], w.rearrange("(h p) d -> p h d", p=P)).then_inc(s_w, 16)
            with nc.allow_non_contiguous_dma(reason="biases, one column each"):
                sp.dma_start(bqk[:, 0], bq.rearrange("(h p) -> p h", p=P)).then_inc(s_small, 16)
                sp.dma_start(bqk[:, 1], bk.rearrange("(h p) -> p h", p=P)).then_inc(s_small, 16)
            for j in range(2):
                sp.dma_start(bv_row[:, j], bv.rearrange("(a d) -> a d", a=1).partition_broadcast(P)).then_inc(s_small, 16)
            sp.dma_start(w1[:, :, :], W.rearrange("(k p) d -> p k d", p=P)).then_inc(s_small, 16)
            sp.dma_start(xin[:, 1], x_g[1]).then_inc(s_xin[1], 16)

            def x_group(g, par):
                sp.wait_ge(s_hT_ps, g - 1)
                sp.dma_start(xin[:, par], x_g[g]).then_inc(s_xin[par], 16)

            with sp.Fori(0, (NG - 2) // 2) as i:
                x_group(2 * i + 2, 0)
                x_group(2 * i + 3, 1)

            def x_pair(s, par, view):
                wait(sp, s_x1, 2 * s - 2)
                sp.dma_start(xt[:, par], view[s]).then_inc(s_xt[par], 16)

            def x1_store(s, view):
                sp.wait_ge(s_x1, 2 * s + 2)
                sp.dma_start(view[s], x1[:, :, :]).then_inc(s_x1_out, 16)

            def mean_adj(t):
                sp.dma_start(adjL[:, t % 2], adj_t[t]).then_inc(d_adj[t % 2], 16)

            sp.wait_ge(s_fast, 1)
            flag = sp.value_load(fast[0:1, 0:1], min_val=0, max_val=1)
            with sp.If(flag > 0):
                sp.dma_start(adjU[:, HALF:N], adj_t[HT][:, HALF:N]).then_inc(s_window, 16)
                sp.dma_start(adjU[:, 0:HALF], adj_t[HT][:, 0:HALF]).then_inc(s_beside, 16)
                sp.dma_start(adjL[:, 0], adj_t[0]).then_inc(s_adjL[0], 16)
                sp.wait_ge(s_v_ps, 2 * NG)

                def step(s, par):
                    if not is_step(s, HT - 1):
                        sp.wait_ge(s_qk_used, (HC + 1) * s + HC)
                        sp.dma_start(adjU[:, HALF:N], adj_t[s + HT + 1][:, HALF:N]).then_inc(s_window, 16)
                        wait(sp, s_expL, s)
                        sp.dma_start(adjL[:, 1 - par], adj_t[s + 1]).then_inc(s_adjL[1 - par], 16)
                    if after(s, 1):
                        x1_store(s - 2, x1_halves)
                    x_pair(s, par, x_halves)
                    if not is_step(s, HT - 1):
                        sp.wait_ge(s_expB, s + 1)
                        sp.sem_inc(s_sync_seen, 1)
                        sp.dma_start(adjU[:, 0:HALF], adj_t[s + HT + 1][:, 0:HALF]).then_inc(s_beside, 16)

                pipeline(sp, HT, step, 2, 4)
                x1_store(HT - 2, x1_halves)
                sp.wait_ge(s_expL, HT - 1)
                mean_adj(0)
                sp.wait_ge(s_expL, HT)
                mean_adj(1)
                x1_store(HT - 1, x1_halves)
            with sp.Else():
                sp.wait_ge(s_v_ps, 2 * NG)

                def pair(s, par):
                    x_pair(s, par, x_pairs)
                    for slot in range(2):
                        n = 2 * s + slot
                        wait(sp, s_pT_ps, n * NG)
                        sp.dma_start(adjL[:, 0], adj_t[n]).then_inc(g_adj, 16)
                    x1_store(s, x1_pairs)

                pipeline(sp, HT, pair, 2)
                sp.wait_ge(s_mx, HT)
                mean_adj(0)
                mean_adj(1)

            sp.wait_ge(s_x1_out, 16 * HT)
            sp.wait_ge(s_lo, T)
            def mean_adj_next(t, par):
                sp.wait_ge(d_t_ps, NG * t + NG)
                sp.dma_start(adjL[:, par], adj_t[t + 2]).then_inc(d_adj[par], 16)

            for t in range(4):
                mean_adj_next(t, t % 2)
                sp.dma_start(x1_all[:, t * HT // 2:(t + 1) * HT // 2, :],
                             x1_dram[t * N // 4:(t + 1) * N // 4, :].rearrange("(t p) d -> p t d", p=P))\
                  .then_inc(s_x1_all, 16)
            with sp.Fori(2, HT - 1) as i:
                for par in range(2):
                    mean_adj_next(2 * i + par, par)
            for g in range(NG):
                sp.wait_ge(s_out, g + 1)
                sp.dma_start(out_g[g], res[:, g * BPC:(g + 1) * BPC, :]).then_inc(s_stored, 16)
            sp.wait_ge(s_stored, 16 * NG)

        @block.gpsimd
        def _(pool):
            pool.iota(row_no_i[:, :], pattern=[[P, T]], base=0, channel_multiplier=1).then_inc(s_rows, 1)
            pool.memset(ident[:, :], 0.0).then_inc(s_ident, 1)
            pool.memset(ones_b[:, :], 1.0).then_inc(s_ident, 1)
            pool.wait_ge(s_ident, 2)
            pool.affine_select(out=ident[:, :], in_=ident[:, :], compare_op=ALU.not_equal, fill=1.0, base=0,
                               pattern=[[-1, P]], channel_multiplier=1).then_inc(s_ident, 1)

            pool.wait_ge(s_kq, 2 * KD * NG // 2 + KD)
            pool.wait_ge(s_fast, 1)
            flag = pool.value_load(fast[0:1, 0:1], min_val=0, max_val=1)
            def stage(t):
                always(pool)
                pool.tensor_copy(q_hi[:, :, :].rearrange("p k c -> p (k c)"), qx[:, t, 0:D])
                pool.drain()
                pool.tensor_tensor(q_lo[:, :, :].rearrange("p k c -> p (k c)"), qx[:, t, 0:D],
                                   q_hi[:, :, :].rearrange("p k c -> p (k c)").bitcast(F32), ALU.subtract)\
                    .then_inc(s_q, 1)

            def stage_low(t):
                always(pool)
                pool.tensor_copy(q_low[:, :, :].rearrange("p k c -> p (k c)"), qx[:, t, 0:D]).then_inc(s_q, 1)

            with pool.If(flag > 0):
                def stage_pair(s):
                    wait(pool, s_qk, (HC + 1) * s)
                    stage(s + HT)
                    stage_low(s)

                def step(s, par):
                    if not is_step(s, HT - 1):
                        stage_pair(s + 1)
                    pool.wait_ge(s_own, s + 1)
                    always(pool)
                    pool.tensor_tensor(own[:, par, :], own[:, par, :], same[:, par, :], ALU.mult).then_inc(s_own_m, 1)

                stage_pair(0)
                pool.wait_ge(s_kq, 2 * KD * NG)
                pipeline(pool, HT, step)
            with pool.Else():
                def pair(s, par):
                    for slot in range(2):
                        n = 2 * s + slot
                        wait(pool, g_qk, NG * n)
                        stage(n)
                        stage_low(n)

                pipeline(pool, HT, pair)

        @block.tensor
        def _(pe):
            pe.wait_ge(s_ident, 3)
            pe.wait_ge(s_w, 16 * 3)
            for n in range(3):
                for h in range(KD):
                    for k in range(KD):
                        last = pe.transpose(bank[2 + n][:, k * D + h * P:k * D + (h + 1) * P],
                                            w_raw[:, n, h, k * P:(k + 1) * P], ident[:, :])
                last.then_inc(s_wt_ps, 1)
            def graph_numbers(g):
                pe.wait_ge(s_diag, g + 1)
                pe.wait_ge(s_kq, 4 * g + 1)
                pe.matmul(bank[2][:, :], ones_b[:, :], diag[:, g % 2, :], start=True, stop=True)\
                  .then_inc(s_grow_ps, 1)

            def turn_h(g, par):
                pe.wait_ge(s_norm, g + 1)
                wait(pe, s_hT, KD * g)
                for k in range(KD):
                    for j in range(BPC):
                        last = pe.transpose(bank[k][:, j * P:(j + 1) * P], xin[:, par, j, k * P:(k + 1) * P],
                                            ident[:, :])
                last.then_inc(s_hT_ps, 1)

            def three(dst, a, b, a_cols, b_cols, k_first=True, k_last=True):
                for n, (i, j) in enumerate(((0, 0), (0, 1), (1, 0))):
                    last = pe.matmul(dst, a[i][a_cols], b[j][b_cols], start=(k_first and n == 0),
                                     stop=(k_last and n == 2))
                return last

            hT_parts, wT_parts = (hT_hi, hT_lo), (wT_hi, wT_lo)
            every = slice(None)

            def project(g, par):
                pe.wait_ge(s_hT, KD * (g + 1))
                for w in range(2):
                    for h in range(KD):
                        i = w * KD + h
                        wait(pe, s_kq, 4 * g + i - 3)
                        if i == 0:
                            wait(pe, s_grow, g)
                        if w == 1 and g > NG // 2:
                            pe.wait_ge(s_key_lo, KD * (g - NG // 2 - 1) + h + 1)
                        for k in range(KD):
                            last = three(bank[2 + i][:, :], wT_parts, hT_parts,
                                         (every, w, k, slice(h * P, (h + 1) * P)), (every, par, k, every),
                                         k == 0, k == KD - 1)
                        last.then_inc(s_kq_ps, 1)

                if g < NG - 1:
                    turn_h(g + 1, 1 - par)
                for b in range(2):
                    if b == 1:
                        graph_numbers(g)
                    wait(pe, s_v, 2 * g + b - 1)
                    for j in range(2):
                        for k in range(KD):
                            last = three(bank[6 + b][:, j * D:(j + 1) * D], hT_parts, wT_parts,
                                         (every, par, k, slice((2 * b + j) * P, (2 * b + j + 1) * P)),
                                         (every, 2, k, every), k == 0, k == KD - 1)
                    last.then_inc(s_v_ps, 1)

            turn_h(0, 0)
            pe.wait_ge(s_wt, 3)
            for g in range(NG - 1):
                project(g, g % 2)
            pe.wait_ge(s_fast, 1)
            flag = pe.value_load(fast[0:1, 0:1], min_val=0, max_val=1)
            project(NG - 1, (NG - 1) % 2)
            pe.wait_ge(s_grow, NG)
            pe.wait_ge(s_kq, 4 * NG)
            pe.wait_ge(s_key_lo, KD * NG // 2)
            pe.wait_ge(s_small, 16 * 5)
            q_parts, keysU_parts = (q_hi, q_lo), (keysU_hi, keysU_lo)

            def turn_cent(s):
                pe.wait_ge(s_cent, 2 * s + 2)
                wait(pe, s_mx, s)
                for slot in range(2):
                    for k in range(KD):
                        last = pe.transpose(bank[7][:, (slot * KD + k) * P:(slot * KD + k + 1) * P],
                                            cent[:, slot, k * P:(k + 1) * P], ident[:, :])
                last.then_inc(s_cT_ps, 1)

            def product(s):
                pe.wait_ge(s_cT, s + 1)
                for slot in range(2):
                    for k in range(KD):
                        last = pe.matmul(bank[7][:, slot * D:(slot + 1) * D], centT[:, slot, k, :], w1[:, k, :],
                                         start=(k == 0), stop=(k == KD - 1))
                last.then_inc(s_mx_ps, 1)

            with pe.If(flag > 0):
                def scores_of(s, par):
                    pe.wait_ge(s_q, 2 * s + 2)
                    for c in range(HC + 1):
                        b = 1 + (par * (HC + 1) + c) % 2
                        wait(pe, s_qk_used, (HC + 1) * s + c - 1)
                        for k in range(KD):
                            if c < HC:
                                last = three(bank[b][:, :], q_parts, keysU_parts, (every, k, every),
                                             (every, k, slice(c * CH, (c + 1) * CH)), k == 0, k == KD - 1)
                            else:
                                last = pe.matmul(bank[b][:, 0:P], q_low[:, k, :], keysL_t[:, k, s, :],
                                                 start=(k == 0), stop=(k == KD - 1))
                        last.then_inc(s_qk, 1)

                def turn(s, par, c):
                    b = (par * (HC + 1) + c) % 2
                    if c == 0:
                        pe.wait_ge(s_expU, s + 1)
                    if c == HC:
                        pe.wait_ge(s_own_m, s + 1)
                    wait(pe, s_pT, (HC + 1) * s + c - 1)
                    if c < HC:
                        for j in range(BPC):
                            last = pe.transpose(bank[3 + b][:, j * P:(j + 1) * P],
                                                scores[:, par, (c * BPC + j) * P:(c * BPC + j + 1) * P], ident[:, :])
                    else:
                        last = pe.transpose(bank[3 + b][:, 0:P], own[:, par, :], ident[:, :])
                    last.then_inc(s_pT_ps, 1)

                def weigh(s, par, c):
                    b = (par * (HC + 1) + c) % 2
                    pe.wait_ge(s_pT, (HC + 1) * s + c + 1)
                    if c < HC:
                        if c == 0:
                            wait(pe, s_x1, 2 * s - 2)
                        for j in range(BPC):
                            last = pe.matmul(bank[UPPER_BANK[par]][:, 0:D], probT[:, b, j, :],
                                             values[:, HT + c * BPC + j, :],
                                             start=(c == 0 and j == 0), stop=(c == HC - 1 and j == BPC - 1))
                    else:
                        wait(pe, s_x1, 2 * s)
                        last = pe.matmul(bank[6][:, 0:D], probT[:, b, 0, :], values[:, s, :], start=True, stop=True)
                    last.then_inc(s_pv, 1)

                def step(s, par):
                    if not is_step(s, HT - 1):
                        scores_of(s + 1, 1 - par)
                    turn(s, par, 0)
                    turn(s, par, 1)
                    if after(s, 1):
                        product(s - 2)
                    for c in range(HC + 1):
                        weigh(s, par, c)
                        if c + 2 <= HC:
                            turn(s, par, c + 2)
                    if after(s, 0):
                        turn_cent(s - 1)

                scores_of(0, 0)
                pe.wait_ge(s_v, 2 * NG)
                pipeline(pe, HT, step, 2, 4)
                product(HT - 2)
                turn_cent(HT - 1)
                product(HT - 1)
            with pe.Else():
                pe.wait_ge(s_v, 2 * NG)

                def pair(s, par):
                    for slot in range(2):
                        n = 2 * s + slot
                        pe.wait_ge(s_q, 2 * n + 2)
                        for c in range(NG):
                            wait(pe, g_qk_used, NG * n + c - 1)
                            for k in range(KD):
                                if c < NG // 2:
                                    last = pe.matmul(bank[1 + c % 2][:, :], q_low[:, k, :],
                                                     keysL[:, k, c * CH:(c + 1) * CH], start=(k == 0),
                                                     stop=(k == KD - 1))
                                else:
                                    cu = c - NG // 2
                                    last = three(bank[1 + c % 2][:, :], q_parts, keysU_parts, (every, k, every),
                                                 (every, k, slice(cu * CH, (cu + 1) * CH)), k == 0, k == KD - 1)
                            last.then_inc(g_qk, 1)
                        pe.wait_ge(g_mask, n + 1)
                        for c in range(NG):
                            wait(pe, s_pT, NG * n + c - 1)
                            for j in range(BPC):
                                last = pe.transpose(bank[3 + c % 2][:, j * P:(j + 1) * P],
                                                    adjL[:, 0, (c * BPC + j) * P:(c * BPC + j + 1) * P], ident[:, :])
                            last.then_inc(s_pT_ps, 1)
                            pe.wait_ge(s_pT, NG * n + c + 1)
                            if c == 0:
                                wait(pe, s_x1, n - 1)
                            for j in range(BPC):
                                last = pe.matmul(bank[5 + slot][:, 0:D], probT[:, c % 2, j, :],
                                                 values[:, c * BPC + j, :],
                                                 start=(c == 0 and j == 0), stop=(c == NG - 1 and j == BPC - 1))
                            last.then_inc(s_pv, 1)
                    turn_cent(s)
                    product(s)

                pipeline(pe, HT, pair)

            pe.wait_ge(s_x1, T)

            def turn_adj(t, par, g):
                if g == 0:
                    pe.wait_ge(d_adj[par], turns(t, par))
                wait(pe, d_lo, NG * t + g - 3)
                rows = group_order(t)[g]
                for j in range(BPC):
                    last = pe.transpose(bank[g % 4][:, j * P:(j + 1) * P],
                                        adjL[:, par, (rows * BPC + j) * P:(rows * BPC + j + 1) * P], ident[:, :])
                last.then_inc(d_t_ps, 1)

            def mean_part(t, par, g):
                if g == 0:
                    wait(pe, d_nom, t - 1)
                if is_step(t, 0):
                    pe.wait_ge(s_lo, BPC * (g + 1))
                    if g == NG - 2:
                        pe.wait_ge(s_edge, 2)
                pe.wait_ge(d_lo, NG * t + g + 1)
                rows = group_order(t)[g]
                for j in range(BPC):
                    last = three(bank[4 + par][:, 0:XW], (adjT_hi, adjT_lo), (X_hi, X_lo), (every, g % 4, j, every),
                                 (every, rows * BPC + j, every), g == 0 and j == 0, g == NG - 1 and j == BPC - 1)
                last.then_inc(d_mm, 1)

            def mean_tile(t, par):
                for g in range(NG):
                    turn_adj(t, par, g)
                    if g >= 2:
                        mean_part(t, par, g - 2)
                    elif after(t, 0):
                        mean_part(t - 1, 1 - par, NG - 2 + g)

            pe.wait_ge(s_edge, 1)
            pipeline(pe, T, mean_tile, 4)
            mean_part(T - 1, 1, NG - 2)
            mean_part(T - 1, 1, NG - 1)

        @block.scalar
        def _(act):
            def deviation(g):
                act.wait_ge(s_var, g + 1)
                act.activation(rstd[:, :], mv[:, :, 1], ACT.Sqrt, bias=ln_eps[:, 0:1]).then_inc(s_std, 1)

            def relu_h(g, par):
                act.wait_ge(s_hT_ps, g + 1)
                wait(act, s_v_ps, 2 * g - 2)
                for k in range(KD):
                    act.activation(hT_hi[:, par, k, :], bank[k][:, :], ACT.Relu).then_inc(s_hT_hi, 1)

            def keys_queries(g):
                for w in range(2):
                    for h in range(KD):
                        act.wait_ge(s_kq_ps, 4 * g + w * KD + h + 1)
                        src = bank[2 + w * KD + h][:, :]
                        gu = g - NG // 2
                        if w == 0:
                            ins = act.activation(qx_v[:, g, :, h * P:(h + 1) * P],
                                                 src.rearrange("p (j c) -> p j c", j=BPC), ACT.Identity,
                                                 bias=bqk[:, 0, h:h + 1], scale=HALF_SCALE)
                        elif gu < 0:
                            ins = act.activation(keysL[:, h, g * CH:(g + 1) * CH], src, ACT.Identity,
                                                 bias=bqk[:, 1, h:h + 1])
                        else:
                            ins = act.activation(keysU_hi[:, h, gu * CH:(gu + 1) * CH], src, ACT.Identity,
                                                 bias=bqk[:, 1, h:h + 1])
                        ins.then_inc(s_kq, 1)

            def project(g, par):
                if 0 < g < NG - 1:
                    deviation(g + 1)
                keys_queries(g)
                if g < NG - 1:
                    relu_h(g + 1, 1 - par)
                act.wait_ge(s_grow_ps, g + 1)
                act.copy(graph_row[:, g * CH:(g + 1) * CH], bank[2][:, :]).then_inc(s_grow, 1)

            deviation(0)
            for n in range(3):
                act.wait_ge(s_wt_ps, n + 1)
                act.copy(wT_hi[:, n].rearrange("p k d -> p (k d)"), bank[2 + n][:, :]).then_inc(s_wt_hi, 1)
            relu_h(0, 0)
            act.wait_ge(s_const, 1)
            deviation(1)
            for g in range(NG):
                project(g, g % 2)

            def cent_copy(s):
                act.wait_ge(s_cT_ps, s + 1)
                act.copy(centT[:, :, :, :].rearrange("p s k c -> p (s k c)"), bank[7][:, :]).then_inc(s_cT, 1)

            def cent_squares(s, sums):
                act.wait_ge(s_cent, 2 * s + 2)
                always(act)
                for slot in range(2):
                    last = act.activation(junk[:, slot], cent[:, slot], ACT.Square, accum_out=sq2[:, slot:slot + 1])
                last.then_inc(s_csq, 1)
                act.drain()
                act.copy(sums[:, :, s], sq2[:, 0:2])

            def product_out(s, sums, place_of):
                act.wait_ge(s_mx_ps, s + 1)
                always(act)
                for slot in range(2):
                    act.activation(junk[:, 2 + slot], bank[7][:, slot * D:(slot + 1) * D], ACT.Square,
                                   accum_out=sq2[:, 2 + slot:3 + slot])
                act.copy(place_of[:, :, s, 0:D], bank[7][:, :].rearrange("p (h d) -> p h d", h=2)).then_inc(s_mx, 1)
                act.drain()
                act.copy(sums[:, :, s], sq2[:, 2:4]).then_inc(s_msq, 1)

            done = [0]

            def asked():
                done[0] += 1
                act.wait_ge(s_f, done[0])

            def point_function(n, cols):
                asked()
                fn, src, dst = POINT_FUNCTIONS[n]
                if src == "squares":
                    for a in range(3):
                        last = act.activation(halves(roots[:, a])[cols], halves(point_sq[:, a])[cols], fn)
                    last.then_inc(s_fa, 1)
                else:
                    act.activation(halves(v[dst][:, :])[cols], halves(v[src][:, :])[cols], fn).then_inc(s_fa, 1)

            def points_high(n):
                g = POINT_GROUPS[n]
                for t in range(g * BPC, (g + 1) * BPC):
                    act.activation(X_hi[:, t, 0:D], qx[:, t, 0:D], ACT.Copy, scale=v[8][:, t:t + 1]).then_inc(s_hi, 1)

            act.wait_ge(s_fast, 1)
            flag = act.value_load(fast[0:1, 0:1], min_val=0, max_val=1)
            with act.If(flag > 0):
                def exp_upper_rest(s, par):
                    act.wait_ge(s_maxU, s + 1)
                    act.activation(adjU[:, 0:HALF], adjU[:, 0:HALF], ACT.Exp, scale=2.0 * FAR,
                                   bias=neg_top[:, par, 1:2], accum_out=esum[:, par, 1, 0:1]).then_inc(s_expB, 1)

                def exp_upper(s, par):
                    act.activation(scores[:, par, :], scores[:, par, :], ACT.Exp, scale=2.0,
                                   bias=neg_top[:, par, 1:2], accum_out=esum[:, par, 1, 1:2]).then_inc(s_expU, 1)

                def exp_own(s, par):
                    act.wait_ge(s_maxL, s + 1)
                    act.activation(own[:, par, :], own[:, par, :], ACT.Exp, scale=2.0,
                                   bias=neg_top[:, par, 0:1], accum_out=esum[:, par, 0, 1:2]).then_inc(s_own, 1)

                def exp_lower(s, par):
                    act.activation(adjL[:, par], adjL[:, par], ACT.Exp, scale=2.0 * FAR,
                                   bias=neg_top[:, par, 0:1], accum_out=esum[:, par, 0, 0:1]).then_inc(s_expL, 1)

                def step(s, par):
                    last_step = is_step(s, HT - 1)
                    for c in range(HC + 1):
                        if last_step and c >= 2:
                            point_function(c - 2, EARLY_COLS)
                        if c == 2 and after(s, 1):
                            product_out(s - 2, msq_halves, qx_halves)
                        b = (par * (HC + 1) + c) % 2
                        width = CH if c < HC else P
                        act.wait_ge(s_pT_ps, (HC + 1) * s + c + 1)
                        wait(act, s_pv, (HC + 1) * s + c - 1)
                        act.copy(probT[:, b].rearrange("p j c -> p (j c)")[:, 0:width], bank[3 + b][:, 0:width])\
                           .then_inc(s_pT, 1)
                        if c == 2 and not is_step(s, HT - 1):
                            exp_upper_rest(s + 1, 1 - par)
                        if c == 3 and not is_step(s, HT - 1):
                            exp_upper(s + 1, 1 - par)
                    if after(s, 0):
                        cent_copy(s - 1)
                    if last_step:
                        exp_lower(s, par)
                    if after(s, 0):
                        cent_squares(s - 1, csq_halves)
                    if not is_step(s, HT - 1):
                        exp_own(s + 1, 1 - par)
                    if not (is_step(s, HT - 1) or is_step(s, HT - 2)):
                        exp_lower(s + 1, 1 - par)

                exp_upper_rest(0, 0)
                exp_upper(0, 0)
                exp_own(0, 0)
                exp_lower(0, 0)
                pipeline(act, HT, step, 2, 4)
                product_out(HT - 2, msq_halves, qx_halves)
                asked()
                points_high(0)
                cent_copy(HT - 1)
                cent_squares(HT - 1, csq_halves)
                points_high(1)
                points_high(2)
                product_out(HT - 1, msq_halves, qx_halves)
                points_high(3)
            with act.Else():
                def pair(s, par):
                    for slot in range(2):
                        n = 2 * s + slot
                        act.wait_ge(g_max, n + 1)
                        act.activation(adjL[:, 0, :], adjL[:, 0, :], ACT.Exp, scale=2.0, bias=neg_top[:, par, slot:slot + 1],
                                       accum_out=esum[:, par, slot, 0:1]).then_inc(g_exp, 1)
                        for c in range(NG):
                            act.wait_ge(s_pT_ps, NG * n + c + 1)
                            wait(act, s_pv, NG * n + c - 1)
                            act.copy(probT[:, c % 2].rearrange("p j c -> p (j c)"), bank[3 + c % 2][:, :])\
                               .then_inc(s_pT, 1)
                    cent_copy(s)
                    cent_squares(s, csq_pairs)
                    product_out(s, msq_pairs, qx_pairs)

                pipeline(act, HT, pair)
                done[0] = 0
                for n in range(3):
                    point_function(n, EARLY_COLS)
                asked()
                for n in range(4):
                    points_high(n)
            point_function(0, LAST_COLS)

            def function(fn, src, dst, squares, cols):
                asked()
                if src == "squares":
                    act.activation(roots[:, :, cols], squares[:, :, cols], fn).then_inc(s_fa, 1)
                else:
                    act.activation(v[dst][:, cols], v[src][:, cols], fn).then_inc(s_fa, 1)

            def mean_tile(t, par):
                if is_step(t, T - 4):
                    act.drain().then_inc(d_sq, 1)
                for g in range(NG):
                    n = NG * (t - T + 4) + g if after(t, T - 5) and isinstance(t, int) else -1
                    if n in FINISH_GROUPS:
                        function(*FINISH_FUNCTIONS[FINISH_GROUPS.index(n)], mean_sq, slice(0, T - LATE))
                    if is_step(t, 0):
                        if g in (2, 4):
                            point_function(g // 2, LAST_COLS)
                        if g == NG - 2:
                            asked()
                        if g >= 4:
                            points_high(g)
                    act.wait_ge(d_t_ps, NG * t + g + 1)
                    wait(act, d_mm, NG * t + g - 3)
                    act.copy(adjT_hi[:, g % 4].rearrange("p j c -> p (j c)"), bank[g % 4][:, :]).then_inc(d_hi, 1)
                    if g == 3 and after(t, 0):
                        mean_out(t - 1, 1 - par)
                    if g == 7 and after(t, 0):
                        mean_squares(t - 1, 1 - par)

            def mean_out(t, par):
                act.wait_ge(d_mm, NG * t + NG)
                act.copy(nom[:, par, :], bank[4 + par][:, 0:XW]).then_inc(d_nom, 1)

            def mean_squares(t, par):
                act.wait_ge(d_r, t + 1)
                act.activation(junk[:, 0], nom[:, par, 0:D], ACT.Square, scale=rec[:, par:par + 1],
                               accum_out=sq2[:, 0:1])
                act.activation(junk[:, 1], res[:, t, :], ACT.Square, accum_out=sq2[:, 1:2])
                act.drain()
                act.copy(mean_sq[:, 1, bass.ds(t, 1)], sq2[:, 0:1])
                act.copy(mean_sq[:, 2, bass.ds(t, 1)], sq2[:, 1:2])

            pipeline(act, T, mean_tile, 4)
            mean_out(T - 1, 1)
            mean_squares(T - 1, 1)
            act.drain().then_inc(d_sq, 1)
            for fn, src, dst in FINISH_FUNCTIONS:
                function(fn, src, dst, mean_sq, slice(T - LATE, T))

        @block.vector
        def _(dve):
            def statistics(g, par):
                dve.wait_ge(s_xin[par], 16 * (g // 2 + 1))
                for j in range(BPC):
                    dve.bn_stats(bnst[:, j, :], xin[:, par, j, :])
                dve.drain()
                for j in range(BPC):
                    last = dve.bn_aggr(mv[:, j, :], bnst[:, j, :])
                last.then_inc(s_var, 1)

            def normalise(g, par):
                dve.wait_ge(s_std, g + 1)
                dve.reciprocal(rstd[:, :], rstd[:, :])
                dve.drain()
                for j in range(BPC):
                    last = dve.tensor_scalar(xin[:, par, j, :], xin[:, par, j, :], mv[:, j, 0:1], rstd[:, j:j + 1],
                                             ALU.subtract, ALU.mult)
                last.then_inc(s_norm, 1)

            def low_h(g, par):
                for k in range(KD):
                    dve.wait_ge(s_hT_hi, KD * g + k + 1)
                    dve.scalar_tensor_tensor(out=hT_lo[:, par, k, :], in0=bank[k][:, :], scalar=0.0,
                                             in1=hT_hi[:, par, k, :].bitcast(F32), op0=ALU.max,
                                             op1=ALU.subtract).then_inc(s_hT, 1)

            dve.memset(ln_eps[:, :], LN_EPS)
            dve.memset(pushed[:, :], PUSHED_OUT)
            for i in range(HT):
                dve.memset(borders[:, i:i + 1], float((i + 1) * P))
            dve.wait_ge(s_rows, 1)
            dve.tensor_copy(row_no[:, :], row_no_i[:, :])
            dve.wait_ge(s_ident, 3)
            dve.tensor_copy(ident_b[:, :], ident[:, :])
            dve.drain()
            statistics(0, 0)
            normalise(0, 0)
            for n in range(3):
                dve.wait_ge(s_wt_hi, n + 1)
                dve.tensor_tensor(wT_lo[:, n].rearrange("p k d -> p (k d)"), bank[2 + n][:, :],
                                  wT_hi[:, n].rearrange("p k d -> p (k d)").bitcast(F32), ALU.subtract)\
                   .then_inc(s_wt, 1)
            low_h(0, 0)
            dve.wait_ge(s_small, 16 * 5)
            dve.tensor_scalar(bqk[:, 0], bqk[:, 0], HALF_SCALE, None, ALU.mult).then_inc(s_const, 1)
            statistics(1, 1)
            normalise(1, 1)
            dve.wait_ge(s_ptr, 16)
            dve.tensor_copy(ptr_f[:, :], ptr_i[:, :])
            dve.drain()
            dve.tensor_tensor(counts[:, :, :], row_no[:, :].unsqueeze(2).to_broadcast([P, T, NPTR]),
                              ptr_f[:, :].unsqueeze(1).to_broadcast([P, T, NPTR]), ALU.is_ge)
            dve.drain()
            dve.tensor_reduce(graph_col[:, :], counts[:, :, :], AX.X, ALU.add)
            dve.tensor_tensor(border_eq[:, :, :], borders[:, :].unsqueeze(2).to_broadcast([P, HT, NPTR]),
                              ptr_f[:, :].unsqueeze(1).to_broadcast([P, HT, NPTR]), ALU.is_equal)
            dve.tensor_scalar(in_upper[:, :], ptr_f[:, :], float(HALF), None, ALU.is_gt)
            dve.tensor_scalar(below_end[:, :], ptr_f[:, :], float(N), None, ALU.is_lt)
            dve.drain()
            dve.tensor_reduce(border_hit[:, :], border_eq[:, :, :], AX.X, ALU.max)
            dve.tensor_tensor(in_upper[:, :], in_upper[:, :], below_end[:, :], ALU.mult)
            dve.drain()
            dve.tensor_reduce(checks[:, 0:1], border_hit[:, :], AX.X, ALU.add)
            dve.tensor_reduce(checks[:, 1:2], in_upper[:, :], AX.X, ALU.add)
            dve.drain()
            dve.tensor_tensor(checks[:, 2:3], checks[:, 0:1], checks[:, 1:2], ALU.subtract)
            dve.drain()
            dve.tensor_scalar(fast[:, :], checks[:, 2:3], float(HT), None, ALU.is_ge).then_inc(s_fast, 1)

            def diagonal(g):
                wait(dve, s_grow_ps, g - 1)
                for j in range(BPC):
                    t = g * BPC + j
                    last = dve.tensor_scalar(diag[:, g % 2, j * P:(j + 1) * P], ident_b[:, :],
                                             graph_col[:, t:t + 1], None, ALU.mult)
                last.then_inc(s_diag, 1)

            def project(g, par):
                diagonal(g)
                if 0 < g < NG - 1:
                    statistics(g + 1, 1 - par)
                    normalise(g + 1, 1 - par)
                gu = g - NG // 2
                if gu >= 0:
                    for h in range(KD):
                        dve.wait_ge(s_kq, 4 * g + KD + h + 1)
                        dve.scalar_tensor_tensor(out=keysU_lo[:, h, gu * CH:(gu + 1) * CH], in0=bank[2 + KD + h][:, :],
                                                 scalar=bqk[:, 1, h:h + 1],
                                                 in1=keysU_hi[:, h, gu * CH:(gu + 1) * CH].bitcast(F32),
                                                 op0=ALU.add, op1=ALU.subtract).then_inc(s_key_lo, 1)
                if g < NG - 1:
                    low_h(g + 1, 1 - par)
                for b in range(2):
                    dve.wait_ge(s_v_ps, 2 * g + b + 1)
                    dve.tensor_tensor(val_v[:, g, 2 * b:2 * b + 2, :], bank[6 + b][:, :].rearrange("p (j d) -> p j d", j=2),
                                      bv_row[:, :, :], ALU.add).then_inc(s_v, 1)

            for g in range(NG):
                project(g, g % 2)

            def attend(groups, s, par, slot, b):
                dve.wait_ge(s_pv, groups)
                dve.wait_ge(s_xt[par], turns(s, par))
                wait(dve, s_x1_out, 16 * s)
                dve.scalar_tensor_tensor(out=x1[:, slot], in0=bank[b][:, 0:D], scalar=tot[:, slot:slot + 1],
                                         in1=xt[:, par, slot], op0=ALU.mult, op1=ALU.add).then_inc(s_x1, 1)

            def centre(s, var_place):
                dve.drain()
                for slot in range(2):
                    dve.bn_stats(bn1[:, slot, :], x1[:, slot])
                dve.drain()
                for slot in range(2):
                    dve.bn_aggr(mv1[:, slot, :], bn1[:, slot, :])
                dve.drain()
                dve.tensor_copy(var_place[:, :, s], mv1[:, :, 1])
                wait(dve, s_cT_ps, s)
                wait(dve, s_csq, s)
                for slot in range(2):
                    dve.tensor_scalar(cent[:, slot], x1[:, slot], mv1[:, slot, 0:1], 0.0, ALU.subtract, ALU.max)\
                       .then_inc(s_cent, 1)

            taken = [0]

            def function_done():
                taken[0] += 1
                dve.wait_ge(s_fa, taken[0])

            def ts(o, a, s1, s2, op0, op1=ALU.bypass):
                last = dve.tensor_scalar(o, a, s1, s2, op0, op1) if s2 is not None else dve.tensor_scalar(o, a, s1, None, op0)
                return last

            def tt(o, a, b, op):
                return dve.tensor_tensor(o, a, b, op)

            def artanh_start(a, t1, t2):
                ts(t1, a, -1.0, 1.0, ALU.mult, ALU.add)
                ts(t2, a, 1.0, None, ALU.add)
                dve.drain()
                dve.reciprocal(t1, t1)
                dve.drain()
                tt(t1, t1, t2, ALU.mult).then_inc(s_f, 1)

            def artanh_series(a, t2, t3):
                tt(t2, a, a, ALU.mult)
                dve.drain()
                ts(t3, t2, 1.0 / 13, None, ALU.mult)
                for c in (11, 9, 7, 5, 3):
                    dve.drain()
                    dve.scalar_tensor_tensor(out=t3, in0=t3, scalar=1.0 / c, in1=t2, op0=ALU.add, op1=ALU.mult)
                dve.drain()
                dve.scalar_tensor_tensor(out=t3, in0=t3, scalar=1.0, in1=a, op0=ALU.add, op1=ALU.mult)
                ts(t2, a, TINY_ARG, None, ALU.is_lt)

            def artanh_end(o, t1, t2, t3):
                function_done()
                dve.scalar_tensor_tensor(out=t3, in0=t1, scalar=-0.5, in1=t3, op0=ALU.mult, op1=ALU.add)
                dve.drain()
                tt(t3, t3, t2, ALU.mult)
                dve.drain()
                dve.scalar_tensor_tensor(out=o, in0=t1, scalar=0.5, in1=t3, op0=ALU.mult, op1=ALU.add)
                dve.drain()

            V = [a[:, :] for a in v]
            Vh = [halves(a[:, :]) for a in v]

            def points_root(c, pairs):
                dve.wait_ge(s_msq, pairs)
                a = halves(point_sq[:, 0])[c]
                ts(a, a, LN_EPS, None, ALU.add).then_inc(s_f, 1)

            def points_norms(c):
                v0, v1, v2, v3, v4, v5, v6 = (a[c] for a in Vh[0:7])
                function_done()
                dve.reciprocal(v0, halves(roots[:, 0])[c])
                dve.drain()
                tt(v1, v0, halves(roots[:, 1])[c], ALU.mult)
                tt(v4, v0, halves(roots[:, 2])[c], ALU.mult)
                dve.drain()
                ts(v3, v1, EPS, CLIP, ALU.max, ALU.min)
                ts(v1, v1, EPS, None, ALU.max)
                ts(v2, v4, EPS, None, ALU.max)
                ts(v4, v4, EPS, None, ALU.is_gt)
                dve.drain()
                artanh_start(v3, v5, v6)

            def points_series(c):
                v0, v1, v2, v3, v4, v5, v6, v7 = (a[c] for a in Vh[0:8])
                dve.drain()
                artanh_series(v3, v6, v7)
                dve.reciprocal(v1, v1)
                tt(v4, v4, v0, ALU.mult)
                dve.drain()
                tt(v1, v1, v2, ALU.mult)
                dve.reciprocal(v0, v2)
                dve.drain()
                tt(v4, v4, v0, ALU.mult)

            def points_scaled(c):
                v1, v3, v5, v6, v7 = (Vh[i][c] for i in (1, 3, 5, 6, 7))
                artanh_end(v3, v5, v6, v7)
                tt(v3, v3, v1, ALU.mult).then_inc(s_f, 1)

            def points_factor(c):
                v3, v4, v8 = (Vh[i][c] for i in (3, 4, 8))
                dve.drain()
                function_done()
                tt(v3, v3, v4, ALU.mult)
                dve.drain()
                tt(v4, v3, v3, ALU.mult)
                dve.drain()
                tt(v4, v4, halves(point_sq[:, 2])[c], ALU.mult)
                dve.drain()
                ts(v4, v4, -1.0, 1.0, ALU.mult, ALU.add)
                dve.drain()
                dve.reciprocal(v4, v4)
                dve.drain()
                ts(v4, v4, 2.0, 1e-15, ALU.mult, ALU.max)
                dve.drain()
                tt(v8, v3, v4, ALU.mult).then_inc(s_f, 1)

            def points_edge(c):
                v4, v5, v6, v7 = (Vh[i][c] for i in (4, 5, 6, 7))
                ts(v5, v4, -1.0, None, ALU.add)
                dve.memset(v6, 1.0)
                dve.memset(v7, 0.0)
                dve.drain()
                dve.tensor_copy(halves(X_hi[:, :, D])[c], v5)
                dve.tensor_copy(halves(X_hi[:, :, D + 1])[c], v6)
                dve.tensor_copy(halves(X_lo[:, :, D + 1])[c], v7)
                dve.drain()
                tt(halves(X_lo[:, :, D])[c], v5, halves(X_hi[:, :, D])[c].bitcast(F32), ALU.subtract)\
                    .then_inc(s_edge, 1)

            POINT_PARTS = (points_norms, points_series, points_scaled, points_factor, points_edge)

            def points_low(n):
                g = POINT_GROUPS[n]
                for j in range(BPC):
                    t = g * BPC + j
                    dve.wait_ge(s_hi, n * BPC + j + 1)
                    dve.scalar_tensor_tensor(out=X_lo[:, t, 0:D], in0=qx[:, t, 0:D], scalar=v[8][:, t:t + 1],
                                             in1=X_hi[:, t, 0:D].bitcast(F32), op0=ALU.mult,
                                             op1=ALU.subtract).then_inc(s_lo, 1)

            def points_early():
                points_root(EARLY_COLS, EARLY)
                for part in POINT_PARTS:
                    part(EARLY_COLS)

            dve.wait_ge(s_grow, NG)
            flag = dve.value_load(fast[0:1, 0:1], min_val=0, max_val=1)
            with dve.If(flag > 0):
                def scores_upper(s, par):
                    dve.wait_ge(s_window, 16 * s + 16)
                    wait(dve, s_pT_ps, (HC + 1) * (s - 2) + HC)
                    for c in range(HC):
                        dve.wait_ge(s_qk, (HC + 1) * s + c + 1)
                        dve.sem_inc(s_seen, 1)
                        dve.tensor_tensor_reduce(out=scores[:, par, c * CH:(c + 1) * CH],
                                                 in0=adjU[:, HALF + c * CH:HALF + (c + 1) * CH],
                                                 in1=bank[1 + (par * (HC + 1) + c) % 2][:, :], scale=1.0,
                                                 scalar=-3.0e38, op0=ALU.add, op1=ALU.max,
                                                 accum_out=mx[:, c:c + 1]).then_inc(s_qk_used, 1)

                def scores_lower(s, par):
                    wait(dve, s_own_m, s - 1)
                    dve.tensor_scalar(same[:, par, :], graph_t[:, s, :], graph_col[:, bass.ds(s, 1)], None, ALU.is_equal)
                    dve.drain()
                    dve.tensor_scalar(factor[:, :], same[:, par, :], 1.0 - FAR, FAR, ALU.mult, ALU.add)
                    dve.wait_ge(s_qk, (HC + 1) * s + HC + 1)
                    dve.tensor_tensor(near_part[:, :], same[:, par, :], bank[1 + (par * (HC + 1) + HC) % 2][:, 0:P],
                                      ALU.mult).then_inc(s_qk_used, 1)

                def maximum(par, slot, done):
                    dve.drain()
                    dve.scalar_tensor_tensor(out=top[:, :], in0=least[:, :], scalar=FAR, in1=top[:, :],
                                             op0=ALU.mult, op1=ALU.max)
                    dve.drain()
                    dve.tensor_scalar(neg_top[:, par, slot:slot + 1], top[:, :], -2.0, None, ALU.mult).then_inc(done, 1)

                def maximum_upper(s, par):
                    dve.wait_ge(s_beside, 16 * s + 16)
                    dve.tensor_reduce(least[:, :], adjU[:, 0:HALF], AX.X, ALU.min)
                    dve.tensor_reduce(top[:, :], mx[:, 0:HC], AX.X, ALU.max)
                    maximum(par, 1, s_maxU)

                def maximum_lower(s, par):
                    dve.wait_ge(s_adjL[par], turns(s, par))
                    dve.tensor_tensor(far_part[:, :], adjL_t[:, par, s, :], factor[:, :], ALU.mult)
                    dve.drain()
                    dve.tensor_copy(adjL_t[:, par, s, :], pushed[:, :])
                    dve.drain()
                    wait(dve, s_pT_ps, (HC + 1) * (s - 1))
                    dve.sem_inc(s_seen, 1)
                    dve.tensor_tensor_reduce(out=own[:, par, :], in0=far_part[:, :], in1=near_part[:, :], scale=1.0,
                                             scalar=-3.0e38, op0=ALU.add, op1=ALU.max, accum_out=top[:, :])
                    dve.tensor_reduce(least[:, :], adjL[:, par], AX.X, ALU.min)
                    maximum(par, 0, s_maxL)

                def sums(s, par):
                    dve.wait_ge(s_expL, s + 1)
                    dve.tensor_tensor(tot[:, :], esum[:, par, :, 0], esum[:, par, :, 1], ALU.add)
                    dve.drain()
                    dve.reciprocal(tot[:, :], tot[:, :])
                    dve.drain()

                def tiles_out(s, par):
                    attend((HC + 1) * s + HC, s, par, 1, UPPER_BANK[par])
                    attend((HC + 1) * s + HC + 1, s, par, 0, 6)
                    centre(s, var_halves)

                def step(s, par):
                    if not is_step(s, HT - 1):
                        scores_upper(s + 1, 1 - par)
                    if after(s, 0):
                        sums(s - 1, 1 - par)
                    if not is_step(s, HT - 1):
                        scores_lower(s + 1, 1 - par)
                        maximum_upper(s + 1, 1 - par)
                    if after(s, 0):
                        tiles_out(s - 1, 1 - par)
                    if not is_step(s, HT - 1):
                        maximum_lower(s + 1, 1 - par)

                scores_upper(0, 0)
                scores_lower(0, 0)
                maximum_upper(0, 0)
                maximum_lower(0, 0)
                pipeline(dve, HT, step, 2, 4)
                points_early()
                sums(HT - 1, 1)
                tiles_out(HT - 1, 1)
                for n in range(4):
                    points_low(n)
            with dve.Else():
                def pair(s, par):
                    for slot in range(2):
                        n = 2 * s + slot
                        dve.wait_ge(g_adj, 16 * n + 16)
                        for c in range(NG):
                            cols = slice(c * CH, (c + 1) * CH)
                            dve.tensor_scalar(mask_c[:, :], graph_row[:, cols], graph_col[:, bass.ds(n, 1)], None, ALU.is_equal)
                            dve.drain()
                            dve.tensor_scalar(factor_c[:, :], mask_c[:, :], 1.0 - FAR, FAR, ALU.mult, ALU.add)
                            dve.wait_ge(g_qk, NG * n + c + 1)
                            dve.tensor_tensor(near_c[:, :], mask_c[:, :], bank[1 + c % 2][:, :], ALU.mult).then_inc(g_qk_used, 1)
                            dve.drain()
                            dve.tensor_tensor(adjL[:, 0, cols], adjL[:, 0, cols], factor_c[:, :], ALU.mult)
                            dve.drain()
                            dve.tensor_tensor_reduce(out=adjL[:, 0, cols], in0=adjL[:, 0, cols], in1=near_c[:, :], scale=1.0,
                                                     scalar=-3.0e38, op0=ALU.add, op1=ALU.max, accum_out=mx[:, c:c + 1])
                            dve.drain()
                        dve.tensor_reduce(top[:, :], mx[:, 0:NG], AX.X, ALU.max)
                        dve.drain()
                        dve.tensor_scalar(neg_top[:, par, slot:slot + 1], top[:, :], -2.0, None, ALU.mult).then_inc(g_max, 1)
                        dve.wait_ge(g_exp, n + 1)
                        for c in range(NG):
                            cols = slice(c * CH, (c + 1) * CH)
                            dve.tensor_scalar(mask_c[:, :], graph_row[:, cols], graph_col[:, bass.ds(n, 1)], None, ALU.is_equal)
                            dve.drain()
                            dve.tensor_tensor(adjL[:, 0, cols], adjL[:, 0, cols], mask_c[:, :], ALU.mult)
                            dve.drain()
                        dve.drain().then_inc(g_mask, 1)
                        dve.reciprocal(tot[:, slot:slot + 1], esum[:, par, slot, 0:1])
                        dve.drain()
                        attend(NG * n + NG, s, par, slot, 5 + slot)
                    centre(s, var_pairs)

                pipeline(dve, HT, pair)
                taken[0] = 0
                points_early()
                for n in range(4):
                    points_low(n)

            points_root(LAST_COLS, HT)
            def finish_root(c):
                ts(mean_sq[:, 0, c], mean_sq[:, 1, c], -1.0, 1.0, ALU.mult, ALU.add)
                dve.drain()
                ts(mean_sq[:, 0, c], mean_sq[:, 0, c], EPS, None, ALU.max).then_inc(s_f, 1)

            def finish_mean(c):
                function_done()
                ts(V[0][:, c], roots[:, 0, c], 1.0, None, ALU.add)
                dve.drain()
                dve.reciprocal(V[0][:, c], V[0][:, c])
                dve.drain()
                tt(V[1][:, c], V[0][:, c], roots[:, 1, c], ALU.mult)
                dve.drain()
                ts(V[2][:, c], V[1][:, c], EPS, CLIP, ALU.max, ALU.min)
                ts(V[1][:, c], V[1][:, c], EPS, None, ALU.max)
                dve.drain()
                artanh_start(V[2][:, c], V[5][:, c], V[6][:, c])

            def finish_series(c):
                dve.drain()
                artanh_series(V[2][:, c], V[6][:, c], V[7][:, c])
                dve.reciprocal(V[1][:, c], V[1][:, c])
                dve.drain()
                tt(V[0][:, c], V[0][:, c], V[1][:, c], ALU.mult)

            def finish_scaled(c):
                artanh_end(V[2][:, c], V[5][:, c], V[6][:, c], V[7][:, c])
                tt(V[2][:, c], V[2][:, c], alpha[:, c], ALU.mult).then_inc(s_f, 1)

            def finish_product(c):
                function_done()
                tt(V[0][:, c], V[0][:, c], V[2][:, c], ALU.mult)
                dve.drain()
                tt(V[1][:, c], V[0][:, c], roots[:, 1, c], ALU.mult)
                dve.drain()
                ts(V[2][:, c], V[1][:, c], EPS, CLIP, ALU.max, ALU.min)
                ts(V[1][:, c], V[1][:, c], EPS, None, ALU.max)
                dve.drain()
                artanh_start(V[2][:, c], V[5][:, c], V[6][:, c])

            def finish_log(c):
                artanh_end(V[2][:, c], V[5][:, c], V[6][:, c], V[7][:, c])
                tt(V[0][:, c], V[0][:, c], V[2][:, c], ALU.mult)
                dve.drain()
                tt(V[1][:, c], V[0][:, c], roots[:, 2, c], ALU.mult)
                dve.drain()
                ts(V[1][:, c], V[1][:, c], EPS, None, ALU.max).then_inc(s_f, 1)

            def finish_exp(c):
                dve.drain()
                dve.reciprocal(V[2][:, c], V[1][:, c])
                dve.drain()
                tt(V[0][:, c], V[0][:, c], V[2][:, c], ALU.mult)
                dve.drain()
                function_done()
                tt(V[0][:, c], V[0][:, c], V[3][:, c], ALU.mult)

            FINISH_PARTS = (finish_root, finish_mean, finish_series, finish_scaled, finish_product, finish_series,
                            finish_log, finish_exp)

            def add_layer(t):
                last = dve.scalar_tensor_tensor(out=res[:, t, :], in0=res[:, t, :], scalar=v[0][:, t:t + 1],
                                                in1=x1_all[:, t, :], op0=ALU.mult, op1=ALU.add)
                if t % BPC == BPC - 1:
                    last.then_inc(s_out, 1)

            def mean_tile(t, par):
                if is_step(t, T - 4):
                    dve.wait_ge(d_sq, 1)
                if is_step(t, T - 2):
                    dve.drain()
                    dve.wait_ge(s_x1_all, 16 * 4)
                for g in range(NG):
                    if is_step(t, 0) and g >= 4:
                        points_low(g)
                    dve.wait_ge(d_hi, NG * t + g + 1)
                    dve.tensor_tensor(adjT_lo[:, g % 4].rearrange("p j c -> p (j c)"), bank[g % 4][:, :],
                                      adjT_hi[:, g % 4].rearrange("p j c -> p (j c)").bitcast(F32),
                                      ALU.subtract).then_inc(d_lo, 1)
                    if is_step(t, 0) and g < len(POINT_PARTS):
                        POINT_PARTS[g](LAST_COLS)
                    n = NG * (t - T + 4) + g if after(t, T - 5) and isinstance(t, int) else -1
                    if n in range(0, 2 * NG, 2):
                        FINISH_PARTS[n // 2](slice(0, T - LATE))
                    if n >= 2 * NG:
                        n -= 2 * NG
                        for done in range((T - LATE) * n // (2 * NG), (T - LATE) * (n + 1) // (2 * NG)):
                            add_layer(done)
                    if g == 5 and after(t, 0):
                        mean_relu(t - 1, 1 - par)

            def mean_relu(t, par):
                dve.wait_ge(d_nom, t + 1)
                ts(sgn[:, :], nom[:, par, D:D + 2], 0.0, 2.0, ALU.is_ge, ALU.mult)
                dve.drain()
                ts(sgn[:, :], sgn[:, :], -1.0, None, ALU.add)
                dve.drain()
                tt(size[:, :], nom[:, par, D:D + 2], sgn[:, :], ALU.mult)
                dve.drain()
                ts(rec[:, par:par + 1], size[:, 0:1], EPS, None, ALU.max)
                dve.tensor_copy(alpha[:, bass.ds(t, 1)], size[:, 1:2])
                dve.drain()
                dve.reciprocal(rec[:, par:par + 1], rec[:, par:par + 1])
                dve.drain()
                dve.scalar_tensor_tensor(out=turn[:, 0:1], in0=sgn[:, 0:1], scalar=sgn[:, 1:2],
                                         in1=rec[:, par:par + 1], op0=ALU.mult, op1=ALU.mult)
                dve.drain()
                ts(res[:, t, :], nom[:, par, 0:D], turn[:, 0:1], 0.0, ALU.mult, ALU.max).then_inc(d_r, 1)

            pipeline(dve, T, mean_tile, 4)
            mean_relu(T - 1, 1)

            dve.drain()
            dve.wait_ge(d_sq, 2)
            for part in FINISH_PARTS:
                part(slice(T - LATE, T))
            dve.drain()
            for t in range(T - LATE, T):
                add_layer(t)


_INS = ["x", "adj", "L0_gnn_ptr", "L0_gnn_Wq", "L0_gnn_bq", "L0_gnn_Wk", "L0_gnn_bk", "L0_gnn_Wv", "L0_gnn_bv",
        "L1_gnn_W"]


def kernel(**inputs):
    import numpy as _np
    import concourse.bacc as _bacc
    from concourse import mybir as _mybir
    from concourse.bass_utils import run_bass_kernel_spmd as _run

    nc = _bacc.Bacc("TRN2", target_bir_lowering=False, num_devices=1, dynamic_dma_scratch_size=1024)
    arrays, args = {}, []
    for name in _INS:
        a = _np.ascontiguousarray(inputs[name])
        arrays[f"in_{name}"] = a
        args.append(nc.dram_tensor(f"in_{name}", a.shape, _mybir.dt.from_np(a.dtype), kind="ExternalInput").ap())
    shape = inputs["x"].shape
    args.append(nc.dram_tensor("out_x", shape, _mybir.dt.float32, kind="ExternalOutput").ap())
    graph_layers_kernel(nc, *args)
    r = _run(nc, [arrays], core_ids=[0])
    return r.results[0]["out_x"]
```
